# Optimizing a Trainium2 kernel written in Bass

```python
import numpy as np
import jax
import jax.numpy as jnp

def _softmax(x, axis=-1):
    return jax.nn.softmax(x, axis=axis)

def _gelu(x):
    return jax.nn.gelu(x, approximate=True)

def _silu(x):
    return jax.nn.silu(x)

def _sigmoid(x):
    return jax.nn.sigmoid(x)

def _layernorm(x, axis=-1, eps=1e-05):
    m = jnp.mean(x, axis=axis, keepdims=True)
    v = jnp.var(x, axis=axis, keepdims=True)
    return (x - m) / jnp.sqrt(v + eps)

def _scatter_add(tgt, idx, src, axis=0):
    return tgt.at[idx].add(src)

def _segment_sum(src, seg, n):
    return jax.ops.segment_sum(src, seg, n)
kernel_name = 'mk_adj_resnorm_d2_adj_r2_1bdeec'

def setup_inputs(seed: int=0):
    np.random.seed(seed)
    _w = jnp.asarray

    def _rec_inputs():
        import jax
        import jax.numpy as jnp
        _gk = jax.random.key(seed)
        x = 7.22e-05 + 1 * jax.random.normal(jax.random.fold_in(_gk, 1), (32, 256, 128), jnp.float32)
        _w = (1.0 + jnp.arange(256, dtype=jnp.float32)) ** (-0.5)
        _w = _w / _w.mean()
        _pij = jnp.clip(0.015625 * _w[:, None] * _w[None, :], 0.0, 1.0)
        _a = jax.random.uniform(jax.random.fold_in(_gk, 2), (32, 256, 256)) < _pij
        _a = jnp.logical_or(_a, jnp.swapaxes(_a, -1, -2))
        _a = jnp.logical_or(_a, jnp.eye(256, dtype=bool))
        _af = _a.astype(jnp.float32)
        adj = _af
        return (x, adj)
    x, adj = _rec_inputs()

    def _L0_gnn_setup():
        import jax, jax.numpy as jnp
        import numpy as np
        from jax import lax
        DIM = 128
        EPS = 1e-05

        def _bn(h, g, b, m, v):
            scale = g / jnp.sqrt(v + EPS)
            return h * scale[None, :, None] + (b - m * scale)[None, :, None]

        def _conv1d(h, w, pad):
            return lax.conv_general_dilated(h, w, window_strides=(1,), padding=[(pad, pad)], dimension_numbers=('NCH', 'OIH', 'NCH'))
        key = jax.random.key(seed)
        ks = jax.random.split(key, 16)
        bs, n, d = (16, 1024, DIM)
        s = 0.05
        return {'x': jax.random.normal(ks[0], (bs, n, d), jnp.float32), 'mask': jnp.ones((bs, n, n), jnp.float32), 'w_se': jax.random.normal(ks[1], (3, d), jnp.float32) * s, 'b_se': jnp.zeros((3,), jnp.float32), 'conv1_w': jax.random.normal(ks[2], (d, d, 1), jnp.float32) * s, 'bn1_g': jnp.ones((d,), jnp.float32), 'bn1_b': jnp.zeros((d,), jnp.float32), 'bn1_m': jnp.zeros((d,), jnp.float32), 'bn1_v': jnp.ones((d,), jnp.float32), 'conv2_w': jax.random.normal(ks[3], (d, d, 17), jnp.float32) * s, 'bn2_g': jnp.ones((d,), jnp.float32), 'bn2_b': jnp.zeros((d,), jnp.float32), 'bn2_m': jnp.zeros((d,), jnp.float32), 'bn2_v': jnp.ones((d,), jnp.float32), 'w_msg': jax.random.normal(ks[4], (d, d), jnp.float32) * s, 'b_msg': jnp.zeros((d,), jnp.float32), 'w_ih': jax.random.normal(ks[5], (3 * d, 2 * d), jnp.float32) * s, 'b_ih': jnp.zeros((3 * d,), jnp.float32), 'w_hh': jax.random.normal(ks[6], (3 * d, d), jnp.float32) * s, 'b_hh': jnp.zeros((3 * d,), jnp.float32)}
    _L0_gnn_all = _L0_gnn_setup()
    _L0_gnn_in = {k: v for k, v in _L0_gnn_all.items() if k in ('w_se', 'b_se', 'conv1_w', 'bn1_g', 'bn1_b', 'bn1_m', 'bn1_v', 'conv2_w', 'bn2_g', 'bn2_b', 'bn2_m', 'bn2_v', 'w_msg', 'b_msg', 'w_ih', 'b_ih', 'w_hh', 'b_hh')}
    del _L0_gnn_all

    def _L1_gnn_setup():
        import jax, jax.numpy as jnp
        import numpy as np
        D_IN = 128
        D_HID = 256
        key = jax.random.key(seed)
        k1, k2, k3, k4, k5, k6 = jax.random.split(key, 6)
        x = jax.random.normal(k1, (8, 2048, D_IN), dtype=jnp.float32)
        adj = jax.random.uniform(k2, (8, 2048, 2048), dtype=jnp.float32)
        s1 = 1.0 / np.sqrt(D_IN)
        s2 = 1.0 / np.sqrt(D_HID)
        W1 = jax.random.uniform(k3, (D_IN, D_HID), dtype=jnp.float32, minval=-s1, maxval=s1)
        b1 = jax.random.uniform(k4, (D_HID,), dtype=jnp.float32, minval=-s1, maxval=s1)
        W2 = jax.random.uniform(k5, (D_HID, D_IN), dtype=jnp.float32, minval=-s2, maxval=s2)
        b2 = jax.random.uniform(k6, (D_IN,), dtype=jnp.float32, minval=-s2, maxval=s2)
        eps = jnp.zeros((1,), dtype=jnp.float32)
        return {'x': x, 'adj': adj, 'eps': eps, 'W1': W1, 'b1': b1, 'W2': W2, 'b2': b2}
    _L1_gnn_all = _L1_gnn_setup()
    _L1_gnn_in = {k: v for k, v in _L1_gnn_all.items() if k in ('eps', 'W1', 'b1', 'W2', 'b2')}
    del _L1_gnn_all
    return {'x': x, 'adj': adj, 'L0_gnn_w_se': _L0_gnn_in['w_se'], 'L0_gnn_b_se': _L0_gnn_in['b_se'], 'L0_gnn_conv1_w': _L0_gnn_in['conv1_w'], 'L0_gnn_bn1_g': _L0_gnn_in['bn1_g'], 'L0_gnn_bn1_b': _L0_gnn_in['bn1_b'], 'L0_gnn_bn1_m': _L0_gnn_in['bn1_m'], 'L0_gnn_bn1_v': _L0_gnn_in['bn1_v'], 'L0_gnn_conv2_w': _L0_gnn_in['conv2_w'], 'L0_gnn_bn2_g': _L0_gnn_in['bn2_g'], 'L0_gnn_bn2_b': _L0_gnn_in['bn2_b'], 'L0_gnn_bn2_m': _L0_gnn_in['bn2_m'], 'L0_gnn_bn2_v': _L0_gnn_in['bn2_v'], 'L0_gnn_w_msg': _L0_gnn_in['w_msg'], 'L0_gnn_b_msg': _L0_gnn_in['b_msg'], 'L0_gnn_w_ih': _L0_gnn_in['w_ih'], 'L0_gnn_b_ih': _L0_gnn_in['b_ih'], 'L0_gnn_w_hh': _L0_gnn_in['w_hh'], 'L0_gnn_b_hh': _L0_gnn_in['b_hh'], 'L1_gnn_eps': _L1_gnn_in['eps'], 'L1_gnn_W1': _L1_gnn_in['W1'], 'L1_gnn_b1': _L1_gnn_in['b1'], 'L1_gnn_W2': _L1_gnn_in['W2'], 'L1_gnn_b2': _L1_gnn_in['b2']}

def reference(x, adj, L0_gnn_w_se, L0_gnn_b_se, L0_gnn_conv1_w, L0_gnn_bn1_g, L0_gnn_bn1_b, L0_gnn_bn1_m, L0_gnn_bn1_v, L0_gnn_conv2_w, L0_gnn_bn2_g, L0_gnn_bn2_b, L0_gnn_bn2_m, L0_gnn_bn2_v, L0_gnn_w_msg, L0_gnn_b_msg, L0_gnn_w_ih, L0_gnn_b_ih, L0_gnn_w_hh, L0_gnn_b_hh, L1_gnn_eps, L1_gnn_W1, L1_gnn_b1, L1_gnn_W2, L1_gnn_b2):
    import jax
    import jax.numpy as jnp

    def _L0_gnn_ref(x, mask, w_se, b_se, conv1_w, bn1_g, bn1_b, bn1_m, bn1_v, conv2_w, bn2_g, bn2_b, bn2_m, bn2_v, w_msg, b_msg, w_ih, b_ih, w_hh, b_hh):
        import jax, jax.numpy as jnp
        import numpy as np
        from jax import lax
        DIM = 128
        EPS = 1e-05

        def _bn(h, g, b, m, v):
            scale = g / jnp.sqrt(v + EPS)
            return h * scale[None, :, None] + (b - m * scale)[None, :, None]

        def _conv1d(h, w, pad):
            return lax.conv_general_dilated(h, w, window_strides=(1,), padding=[(pad, pad)], dimension_numbers=('NCH', 'OIH', 'NCH'))
        d = x.shape[-1]
        xc = jnp.transpose(x, (0, 2, 1))
        h = _bn(_conv1d(xc, conv1_w, 0), bn1_g, bn1_b, bn1_m, bn1_v)
        h = jax.nn.relu(h)
        h = _bn(_conv1d(h, conv2_w, 8), bn2_g, bn2_b, bn2_m, bn2_v)
        x_conv = jnp.transpose(jax.nn.relu(h + xc), (0, 2, 1))
        s = x @ w_se.T + b_se
        sq = jnp.sum(s * s, axis=-1)
        dist = sq[:, :, None] + sq[:, None, :] - 2.0 * jnp.einsum('bnd,bmd->bnm', s, s)
        A = jnp.exp(-dist) * mask
        msg = jax.nn.relu(x @ w_msg.T + b_msg)
        x_nmp = jnp.einsum('bnm,bmd->bnd', A, msg)
        x_in = jnp.concatenate([x_conv, x_nmp], axis=-1)
        gi = x_in @ w_ih.T + b_ih
        gh = x @ w_hh.T + b_hh
        gi_r, gi_z, gi_n = (gi[..., :d], gi[..., d:2 * d], gi[..., 2 * d:])
        gh_r, gh_z, gh_n = (gh[..., :d], gh[..., d:2 * d], gh[..., 2 * d:])
        r = jax.nn.sigmoid(gi_r + gh_r)
        z = jax.nn.sigmoid(gi_z + gh_z)
        nn_ = jnp.tanh(gi_n + r * gh_n)
        return (1.0 - z) * nn_ + z * x

    def _L1_gnn_ref(x, adj, eps, W1, b1, W2, b2):
        import jax, jax.numpy as jnp
        import numpy as np
        D_IN = 128
        D_HID = 256
        aggregated = jnp.einsum('bnm,bmd->bnd', adj, x)
        h = (1.0 + eps) * x + aggregated
        h = jax.nn.relu(h @ W1 + b1)
        return h @ W2 + b2
    x = _layernorm(x + _L0_gnn_ref(x, adj, L0_gnn_w_se, L0_gnn_b_se, L0_gnn_conv1_w, L0_gnn_bn1_g, L0_gnn_bn1_b, L0_gnn_bn1_m, L0_gnn_bn1_v, L0_gnn_conv2_w, L0_gnn_bn2_g, L0_gnn_bn2_b, L0_gnn_bn2_m, L0_gnn_bn2_v, L0_gnn_w_msg, L0_gnn_b_msg, L0_gnn_w_ih, L0_gnn_b_ih, L0_gnn_w_hh, L0_gnn_b_hh), axis=-1)
    x = _layernorm(x + _L1_gnn_ref(x, adj, L1_gnn_eps, L1_gnn_W1, L1_gnn_b1, L1_gnn_W2, L1_gnn_b2), axis=-1)
    return x

_drawn_inputs = setup_inputs


def setup_inputs(seed=0):
    import zlib

    import numpy as np

    out = dict(_drawn_inputs(seed))
    spreads = {'L0_gnn_b_se': (0.0, 2.0),
     'L0_gnn_bn1_g': (1.0, 0.6),
     'L0_gnn_bn1_b': (0.0, 0.367),
     'L0_gnn_bn1_m': (0.0, 0.356),
     'L0_gnn_bn1_v': (1.0, 0.6),
     'L0_gnn_bn2_g': (1.0, 0.2),
     'L0_gnn_bn2_b': (0.0, 0.528),
     'L0_gnn_bn2_m': (0.0, 0.468),
     'L0_gnn_bn2_v': (1.0, 0.6),
     'L0_gnn_b_msg': (0.0, 0.1),
     'L0_gnn_b_ih': (0.0, 0.1),
     'L0_gnn_b_hh': (0.0, 0.272)}
    factors = {'L1_gnn_b1': 3.565}
    for name, (base, spread) in spreads.items():
        noise = np.random.default_rng([zlib.crc32(name.encode()), seed]).standard_normal(out[name].shape)
        drawn = base * np.exp(spread * noise) if base else spread * noise
        out[name] = jnp.asarray(drawn.astype(out[name].dtype))
    for name, factor in factors.items():
        out[name] = (out[name] * factor).astype(out[name].dtype)
    return out
```

```python
import concourse.bass as bass
from concourse import mybir
from contextlib import ExitStack

F32 = mybir.dt.float32
F32R = mybir.dt.float32r
ALU = mybir.AluOpType
ACT = mybir.ActivationFunctionType

BN_EPS = 1e-5
LN_EPS = 1e-5


def build_program(nc, x, adj, w_se, b_se, conv1_w, bn1_g, bn1_b, bn1_m, bn1_v, conv2_w, bn2_g, bn2_b, bn2_m,
                  bn2_v, w_msg, b_msg, w_ih, b_ih, w_hh, b_hh, eps, W1, b1, W2, b2, out):
    B, N, D = x.shape
    HID = W1.shape[1]
    TAPS = conv2_w.shape[2]
    P = 128
    BP = 2
    PAIRS = B // BP
    M = N // 2
    T = BP * N
    TILES = T // P
    PAD = TAPS // 4
    MP = M + 2 * PAD
    EVEN, ODD = (TAPS + 1) // 2, TAPS // 2
    assert D == P and M == P and HID == 2 * P and TAPS == 17 and PAIRS % 2 == 0 and PAIRS >= 4

    CONV1 = 0
    GATE = 1
    TAP = GATE + 9
    SUM = TAP + TAPS
    BLOCKS = SUM + ODD
    FROM_CONV, FROM_NMP, FROM_X = range(3)
    GATE_R, GATE_Z, GATE_N = range(3)
    S_ROWS = 24
    S_PAD = 32
    SW = P + 4

    x_pairs = x.rearrange("(i b) (m p) d -> i m b p d", b=BP, p=2)
    adj_pairs = adj.rearrange("(i b) (m p) c -> i m b p c", b=BP, p=2)
    out_pairs = out.rearrange("(i b) (m p) d -> i m b p d", b=BP, p=2)

    with ExitStack() as ctx:
        def sb(name, shape, dt=F32):
            return ctx.enter_context(nc.sbuf_tensor(name, shape, dt))

        def sem(name):
            return ctx.enter_context(nc.semaphore(name))

        ps = ctx.enter_context(nc.psum_tensor("ps", [P, 8, 512], F32))
        CA, CB, DA, DB, GR, GNH, GNI, GZ = range(8)

        ident = sb("ident", [P, P])
        conv1_nat = sb("conv1_nat", [P, D])
        conv2_nat = sb("conv2_nat", [P, D, TAPS])
        ih_nat = sb("ih_nat", [P, 3, 2 * D])
        hh_nat = sb("hh_nat", [P, 3, D])
        msg_nat = sb("msg_nat", [P, D])
        se_nat = sb("se_nat", [3, D])
        w_t = sb("w_t", [P, BLOCKS, P])
        w_hi = sb("w_hi", [P, BLOCKS, P], F32R)
        w_lo = sb("w_lo", [P, BLOCKS, P], F32R)
        msgse = sb("msgse", [P, SW])
        gin1 = sb("gin1", [P, HID])
        gin1_hi = sb("gin1_hi", [P, HID], F32R)
        gin1_lo = sb("gin1_lo", [P, HID], F32R)
        gin2 = sb("gin2", [P, 2, D])
        bn = sb("bn", [P, 2, 4])
        bn_r = sb("bn_r", [P, 2])
        bn_scale = sb("bn_scale", [P, 2])
        bn_shift = sb("bn_shift", [P, 2])
        bn_t = sb("bn_t", [P, 2])
        bih = sb("bih", [P, 3])
        bhh = sb("bhh", [P, 3])
        b_rz = sb("b_rz", [P, 2])
        b_rs = sb("b_rs", [P, 1])
        b_zs = sb("b_zs", [P, 1])
        b1_col = sb("b1_col", [P, 2])
        eps_col = sb("eps_col", [P, 1])
        eps1 = sb("eps1", [P, 1])
        bmsg_row = sb("bmsg_row", [P, TILES, D])
        bse_row = sb("bse_row", [P, TILES, 3])
        b2_row = sb("b2_row", [P, TILES, D])
        diag = sb("diag", [P, BP, 2, 2, P])
        minus_half = sb("minus_half", [P, TILES])
        zeros = sb("zeros", [P, TILES, 6])

        x_nat = sb("x_nat", [P, BP, 2, D])
        adj_nat = sb("adj_nat", [P, BP, 2, N])
        xT = [sb(f"xT{k}", [P, T]) for k in range(2)]
        x_hi = sb("x_hi", [P, T], F32R)
        x_lo = sb("x_lo", [P, T], F32R)
        hs = sb("hs", [P, 4, BP, MP])
        hs_hi = sb("hs_hi", [P, 3, BP, MP], F32R)
        hs_lo = sb("hs_lo", [P, 3, BP, MP], F32R)
        msg_pre = sb("msg_pre", [P, TILES, D])
        msg = sb("msg", [P, TILES, D])
        s_nat = sb("s_nat", [P, TILES, 3])
        s_sq = sb("s_sq", [P, TILES, 3])
        lr = sb("lr", [P, TILES, P], F32R)
        left = sb("left", [S_ROWS, T], F32R)
        right = sb("right", [S_ROWS, T], F32R)
        expd = sb("expd", [P, BP, 512])
        amask = sb("amask", [P, BP, 512])
        adjT = [sb(f"adjT{k}", [P, BP, 512]) for k in range(2)]
        base = sb("base", [P, BP, 2, M])
        conv_x = sb("conv_x", [P, T])
        xc_hi = sb("xc_hi", [P, T], F32R)
        xc_lo = sb("xc_lo", [P, T], F32R)
        xn_hi = sb("xn_hi", [P, T], F32R)
        xn_lo = sb("xn_lo", [P, T], F32R)
        r_t = sb("r_t", [P, T])
        z_t = sb("z_t", [P, T])
        r = sb("r", [P, T])
        u = sb("u", [P, T])
        w = sb("w", [P, T])
        n_t = sb("n_t", [P, T])
        d = sb("d", [P, T])
        e = sb("e", [P, T])
        yT = sb("yT", [P, T])
        st1 = sb("st1", [P, TILES, 6])
        mean1 = sb("mean1", [P, TILES])
        half1 = sb("half1", [P, TILES])
        sq1 = sb("sq1", [P, TILES])
        var1 = sb("var1", [P, TILES])
        rstd1 = sb("rstd1", [P, TILES])
        shift1 = sb("shift1", [P, TILES])
        x1 = sb("x1", [P, TILES, D])
        x1b = sb("x1b", [P, TILES, D])
        h_hi = sb("h_hi", [P, T], F32R)
        h_lo = sb("h_lo", [P, T], F32R)
        hidden = sb("hidden", [P, 2, T])
        y2 = sb("y2", [P, TILES, D])
        st2 = sb("st2", [P, TILES, 6])
        mean2 = sb("mean2", [P, TILES])
        half2 = sb("half2", [P, TILES])
        sq2 = sb("sq2", [P, TILES])
        var2 = sb("var2", [P, TILES])
        rstd2 = sb("rstd2", [P, TILES])
        shift2 = sb("shift2", [P, TILES])
        out_nat = sb("out_nat", [P, TILES, D])

        ident_zero = sem("ident_zero")
        ident_ready = sem("ident_ready")
        weights_loaded = sem("weights_loaded")
        small_loaded = sem("small_loaded")
        consts_ready = sem("consts_ready")
        pads_ready = sem("pads_ready")
        bn_rsqrt = sem("bn_rsqrt")
        bn_step = sem("bn_step")
        bn_var = sem("bn_var")
        bn_ready = sem("bn_ready")
        eps_ready = sem("eps_ready")
        bias_step = sem("bias_step")
        conv1_scaled = sem("conv1_scaled")
        conv2_scaled = sem("conv2_scaled")
        w_turned = sem("w_turned")
        w_copied = sem("w_copied")
        w_summed = sem("w_summed")
        w_hi_done = sem("w_hi_done")
        w_split = sem("w_split")
        gin_hi_done = sem("gin_hi_done")
        gin_split = sem("gin_split")
        setup_done = sem("setup_done")

        x_loaded = sem("x_loaded")
        adj_loaded = sem("adj_loaded")
        out_free = sem("out_free")
        x_turned = sem("x_turned")
        conv1_done = sem("conv1_done")
        msg_done = sem("msg_done")
        lr_turned = sem("lr_turned")
        sum_conv_done = sem("sum_conv_done")
        dist_done = sem("dist_done")
        adj_turned = sem("adj_turned")
        y_turned = sem("y_turned")
        conv2_done = sem("conv2_done")
        xn_done = sem("xn_done")
        agg_done = sem("agg_done")
        r_done = sem("r_done")
        z_done = sem("z_done")
        n_done = sem("n_done")
        hidden0_done = sem("hidden0_done")
        hidden1_done = sem("hidden1_done")
        gin_done = sem("gin_done")
        r_tanh = sem("r_tanh")
        z_tanh = sem("z_tanh")
        msg_ready = sem("msg_ready")
        n_ready = sem("n_ready")
        left_ready = sem("left_ready")
        exp_ready = sem("exp_ready")
        x1_ready = sem("x1_ready")
        xc_hi_ready = sem("xc_hi_ready")
        xn_hi_ready = sem("xn_hi_ready")
        h_hi_ready = sem("h_hi_ready")
        hidden_ready = sem("hidden_ready")
        xT_ready = sem("xT_ready")
        h1_ready = sem("h1_ready")
        out_ready = sem("out_ready")
        s_ready = sem("s_ready")
        msg_added = sem("msg_added")
        u_ready = sem("u_ready")
        w_ready = sem("w_ready")
        base_ready = sem("base_ready")
        right_ready = sem("right_ready")
        e_ready = sem("e_ready")
        y_ready = sem("y_ready")
        ln1_stats = sem("ln1_stats")
        ln1_sums = sem("ln1_sums")
        ln1_terms = sem("ln1_terms")
        ln1_var = sem("ln1_var")
        ln1_shift = sem("ln1_shift")
        amask_ready = sem("amask_ready")
        adjT_ready = sem("adjT_ready")
        conv_added = sem("conv_added")
        xc_ready = sem("xc_ready")
        xn_ready = sem("xn_ready")
        h_ready = sem("h_ready")
        x_hi_ready = sem("x_hi_ready")
        x_ready = sem("x_ready")
        u1_hi_ready = sem("u1_hi_ready")
        u1_ready = sem("u1_ready")
        diffs_ready = sem("diffs_ready")
        diff_hi_ready = sem("diff_hi_ready")
        diff_ready = sem("diff_ready")
        y2_ready = sem("y2_ready")
        ln2_stats = sem("ln2_stats")
        ln2_sums = sem("ln2_sums")
        ln2_terms = sem("ln2_terms")
        ln2_var = sem("ln2_var")
        ln2_shift = sem("ln2_shift")
        s_hi_ready = sem("s_hi_ready")
        s_lo_ready = sem("s_lo_ready")
        lr_built = sem("lr_built")
        r_ready = sem("r_ready")
        d_ready = sem("d_ready")
        ln1_rstd = sem("ln1_rstd")
        x1b_ready = sem("x1b_ready")
        ln2_rstd = sem("ln2_rstd")

        N_BIG, N_SMALL = 8, 8 + 3 + 3 + 2 + 1 + 3 * TILES

        block = ctx.enter_context(nc.Block())

        @block.sync
        def _(sp):
            def columns(dst, src):
                for k in range(src.shape[0] // P):
                    sp.dma_start(dst[:, k:k + 1], src[k * P:(k + 1) * P].unsqueeze(1)).then_inc(small_loaded, 16)

            sp.dma_start(x_nat[:], x_pairs[0]).then_inc(x_loaded, 16)
            sp.dma_start(conv1_nat[:], conv1_w.rearrange("o i k -> o (i k)")).then_inc(weights_loaded, 16)
            for which, group in enumerate(((bn1_g, bn1_b, bn1_m, bn1_v), (bn2_g, bn2_b, bn2_m, bn2_v))):
                for k, vector in enumerate(group):
                    columns(bn[:, which, k:k + 1], vector)
            sp.dma_start(ih_nat[:], w_ih.rearrange("(g o) i -> o g i", g=3)).then_inc(weights_loaded, 16)
            sp.dma_start(adj_nat[:], adj_pairs[0]).then_inc(adj_loaded, 16)
            columns(bih, b_ih)
            columns(bhh, b_hh)
            columns(b1_col, b1)
            sp.dma_start(eps_col[:], eps.partition_broadcast(P)).then_inc(small_loaded, 16)
            sp.dma_start(gin1[:], W1).then_inc(weights_loaded, 16)
            sp.dma_start(gin2[:], W2.rearrange("(h p) d -> p h d", h=2)).then_inc(weights_loaded, 16)

            def iteration(i, previous, current, following):
                if current and following:
                    sp.wait_ge(x_turned, i + 1)
                    sp.dma_start(x_nat[:], x_pairs[i + 1]).then_inc(x_loaded, 16)
                    sp.wait_ge(adj_turned, i + 1)
                    sp.dma_start(adj_nat[:], adj_pairs[i + 1]).then_inc(adj_loaded, 16)
                if previous:
                    sp.wait_ge(out_ready, i)
                    sp.dma_start(out_pairs[i - 1], out_nat[:].rearrange("p (b q) d -> p b q d", b=BP))\
                        .then_inc(out_free, 16)

            iteration(0, False, True, True)
            with sp.Fori(1, PAIRS - 2, 2) as t:
                iteration(t, True, True, True)
                iteration(t + 1, True, True, True)
            iteration(PAIRS - 1, True, True, False)
            iteration(PAIRS, True, False, False)
            sp.wait_ge(out_free, 16 * (PAIRS + 1))

        @block.gpsimd
        def _(pool):
            pool.memset(ident[:], 0.0).then_inc(ident_zero, 1)
            pool.memset(out_nat[:, 0, 0:1], 0.0).then_inc(out_free, 16)
            pool.wait_ge(ident_zero, 1)
            pool.affine_select(out=ident[:], in_=ident[:], compare_op=ALU.not_equal, fill=1.0, base=0,
                               pattern=[[-1, P]], channel_multiplier=1).then_inc(ident_ready, 1)
            pool.memset(zeros[:], 0.0)
            pool.memset(minus_half[:], -0.5).then_inc(consts_ready, 1)
            pool.memset(lr[:].bitcast(F32), 0.0).then_inc(consts_ready, 1)
            pool.wait_ge(consts_ready, 2)
            pool.memset(lr[:, :, 18:24].bitcast(F32), 1.0).then_inc(consts_ready, 1)
            pool.memset(lr[:, :, S_PAD + 12:S_PAD + 18].bitcast(F32), 1.0).then_inc(consts_ready, 1)
            pool.wait_ge(bn_var, 1)
            pool.tensor_tensor(bn_r[:], bn_t[:], minus_half[:, 0:2], ALU.pow).then_inc(bn_rsqrt, 1)

            def build_lr(i):
                hi, lo = lr[:, :, 0:3], lr[:, :, 6:9]
                pool.wait_ge(s_ready, i + 1)
                pool.tensor_tensor(s_sq[:], s_nat[:], s_nat[:], ALU.mult)
                pool.tensor_tensor(lr[:, :, 12:15], s_nat[:], s_nat[:], ALU.mult)
                pool.tensor_copy(hi, s_nat[:]).then_inc(s_hi_ready, 1)
                pool.wait_ge(s_hi_ready, i + 1)
                pool.tensor_tensor(lo, s_nat[:], hi.bitcast(F32), ALU.subtract)
                pool.tensor_tensor(lr[:, :, 15:18], s_sq[:], lr[:, :, 12:15].bitcast(F32),
                                   ALU.subtract).then_inc(s_lo_ready, 1)
                pool.tensor_copy(lr[:, :, 3:6], hi.bitcast(F32))
                for at in (0, 6):
                    pool.tensor_scalar(lr[:, :, S_PAD + at:S_PAD + at + 3], hi.bitcast(F32), -2.0, 0.0,
                                       ALU.mult, ALU.add)
                pool.wait_ge(s_lo_ready, i + 1)
                pool.tensor_tensor(lr[:, :, S_PAD + 18:S_PAD + 24], lr[:, :, 12:18].bitcast(F32),
                                   zeros[:], ALU.add)
                pool.tensor_copy(lr[:, :, 9:12], lo.bitcast(F32))
                for at in (3, 9):
                    ins = pool.tensor_scalar(lr[:, :, S_PAD + at:S_PAD + at + 3], lo.bitcast(F32), -2.0, 0.0,
                                             ALU.mult, ALU.add)
                ins.then_inc(lr_built, 1)

            def iteration(i, b, previous, current, following):
                if current:
                    build_lr(i)
                if previous:
                    pool.wait_ge(n_ready, i)
                    pool.tensor_tensor(d[:], xT[1 - b][:], n_t[:], ALU.subtract).then_inc(d_ready, 1)
                    pool.wait_ge(ln1_var, i)
                    pool.tensor_tensor(rstd1[:], var1[:], minus_half[:], ALU.pow).then_inc(ln1_rstd, 1)
                    pool.wait_ge(x1_ready, i)
                    pool.tensor_tensor(x1b[:], x1[:], b2_row[:], ALU.add).then_inc(x1b_ready, 1)
                    pool.wait_ge(ln2_var, i)
                    pool.tensor_tensor(rstd2[:], var2[:], minus_half[:], ALU.pow).then_inc(ln2_rstd, 1)

            pool.wait_ge(consts_ready, 4)
            pool.wait_ge(small_loaded, 16 * N_SMALL)
            iteration(0, 0, False, True, True)
            with pool.Fori(1, PAIRS - 2, 2) as t:
                iteration(t, 1, True, True, True)
                iteration(t + 1, 0, True, True, True)
            iteration(PAIRS - 1, 1, True, True, False)
            iteration(PAIRS, 0, True, False, False)

        @block.scalar
        def _(act):
            act.dma_start(conv2_nat[:], conv2_w).then_inc(weights_loaded, 16)
            act.dma_start(hh_nat[:], w_hh.rearrange("(g o) i -> o g i", g=3)).then_inc(weights_loaded, 16)
            act.dma_start(msg_nat[:], w_msg).then_inc(weights_loaded, 16)
            act.dma_start(se_nat[:], w_se).then_inc(weights_loaded, 16)
            for t in range(TILES):
                act.dma_start(bse_row[:, t, :], b_se.partition_broadcast(P)).then_inc(small_loaded, 16)
                act.dma_start(bmsg_row[:, t, :], b_msg.partition_broadcast(P)).then_inc(small_loaded, 16)
                act.dma_start(b2_row[:, t, :], b2.partition_broadcast(P)).then_inc(small_loaded, 16)

            for k in range(7):
                act.wait_ge(w_turned, k + 1)
                if k < 6:
                    act.activation(w_t[:, 4 * k:4 * k + 4, :], ps[:, k, :], ACT.Copy).then_inc(w_copied, 1)
                else:
                    act.activation(w_t[:, 24:27, :], ps[:, 6, 0:3 * P], ACT.Copy)
                    act.activation(msgse[:, 0:P], ps[:, 6, 3 * P:4 * P], ACT.Copy).then_inc(w_copied, 1)
            act.wait_ge(w_turned, 8)
            act.activation(msgse[:, P:P + 3], ps[:, 7, 0:3], ACT.Copy).then_inc(w_copied, 1)

            def iteration(i, b, previous, current, following):
                if previous:
                    act.wait_ge(r_done, i)
                    act.activation(r_t[:], ps[:, GR, :], ACT.Tanh, bias=b_rs[:], scale=0.5).then_inc(r_tanh, 1)
                    act.wait_ge(z_done, i)
                    act.activation(z_t[:], ps[:, GZ, :], ACT.Tanh, bias=b_zs[:], scale=-0.5)\
                        .then_inc(z_tanh, 1)
                if current:
                    act.wait_ge(msg_added, i + 1)
                    act.activation(msg[:], msg_pre[:], ACT.Relu).then_inc(msg_ready, 1)
                if previous:
                    act.wait_ge(w_ready, i)
                    act.activation(n_t[:], w[:], ACT.Tanh, bias=bih[:, GATE_N:GATE_N + 1]).then_inc(n_ready, 1)
                if current:
                    act.wait_ge(lr_turned, i + 1)
                    act.activation(left[:], ps[0:S_ROWS, DB, :], ACT.Copy).then_inc(left_ready, 1)
                    act.wait_ge(dist_done, i + 1)
                    act.activation(expd[:], ps[:, DA:DB + 1, :], ACT.Exp, scale=-1.0).then_inc(exp_ready, 1)
                if previous:
                    act.wait_ge(ln1_shift, i)
                    for t in range(TILES):
                        ins = act.activation(x1[:, t, :], ps[:, GR, t * P:(t + 1) * P], ACT.Identity,
                                             bias=shift1[:, t:t + 1], scale=rstd1[:, t:t + 1])
                    ins.then_inc(x1_ready, 1)
                if current:
                    act.wait_ge(conv_added, i + 1)
                    act.activation(xc_hi[:], conv_x[:], ACT.Relu).then_inc(xc_hi_ready, 1)
                    act.wait_ge(xn_done, i + 1)
                    act.activation(xn_hi[:], ps[:, GNI, :], ACT.Copy).then_inc(xn_hi_ready, 1)
                if previous:
                    act.wait_ge(agg_done, i)
                    act.activation(h_hi[:], ps[:, GNH, :], ACT.Copy).then_inc(h_hi_ready, 1)
                    act.wait_ge(hidden0_done, i)
                    act.activation(hidden[:, 0, :], ps[:, DA, :], ACT.Relu, bias=b1_col[:, 0:1])
                    act.wait_ge(hidden1_done, i)
                    act.activation(hidden[:, 1, :], ps[:, DB, :], ACT.Relu, bias=b1_col[:, 1:2])\
                        .then_inc(hidden_ready, 1)
                if following:
                    act.wait_ge(x_turned, i + 2)
                    act.activation(xT[1 - b][:], ps[:, CA, :], ACT.Copy).then_inc(xT_ready, 1)
                    act.wait_ge(conv1_done, i + 2)
                    for p in range(2):
                        ins = act.activation(hs[:, p, :, PAD:PAD + M],
                                             ps[:, CA, :].rearrange("c (b p m) -> c b p m", b=BP, p=2)[:, :, p, :],
                                             ACT.Relu, bias=bn_shift[:, 0:1])
                    ins.then_inc(h1_ready, 1)
                if previous:
                    act.wait_ge(ln2_shift, i)
                    act.wait_ge(out_free, 16 * i)
                    for t in range(TILES):
                        ins = act.activation(out_nat[:, t, :], y2[:, t, :], ACT.Identity,
                                             bias=shift2[:, t:t + 1], scale=rstd2[:, t:t + 1])
                    ins.then_inc(out_ready, 1)

            act.wait_ge(setup_done, 1)
            iteration(-1, 1, False, False, True)
            iteration(0, 0, False, True, True)
            with act.Fori(1, PAIRS - 2, 2) as t:
                iteration(t, 1, True, True, True)
                iteration(t + 1, 0, True, True, True)
            iteration(PAIRS - 1, 1, True, True, False)
            iteration(PAIRS, 0, True, False, False)

        @block.vector
        def _(dve):
            dve.memset(hs[:], 0.0)
            dve.memset(msgse[:, P + 3:SW], 0.0)
            dve.memset(diag[:], 0.0).then_inc(pads_ready, 1)
            dve.wait_ge(small_loaded, 16 * N_SMALL)
            dve.tensor_scalar(bn_t[:], bn[:, :, 3], BN_EPS, None, ALU.add).then_inc(bn_var, 1)
            dve.wait_ge(bn_rsqrt, 1)
            dve.tensor_tensor(bn_scale[:], bn[:, :, 0], bn_r[:], ALU.mult).then_inc(bn_step, 1)
            dve.wait_ge(bn_step, 1)
            dve.tensor_tensor(bn_t[:], bn[:, :, 2], bn_scale[:], ALU.mult).then_inc(bn_step, 1)
            dve.wait_ge(weights_loaded, 16 * N_BIG)
            dve.tensor_scalar(conv1_nat[:], conv1_nat[:], bn_scale[:, 0:1], None, ALU.mult)\
                .then_inc(conv1_scaled, 1)
            dve.tensor_scalar(conv2_nat[:], conv2_nat[:], bn_scale[:, 1:2], None, ALU.mult)\
                .then_inc(conv2_scaled, 1)
            dve.wait_ge(bn_step, 2)
            dve.tensor_tensor(bn_shift[:], bn[:, :, 1], bn_t[:], ALU.subtract).then_inc(bn_ready, 1)
            dve.tensor_tensor(b_rz[:], bih[:, 0:2], bhh[:, 0:2], ALU.add).then_inc(bias_step, 1)
            dve.wait_ge(bias_step, 1)
            dve.tensor_scalar(b_rs[:], b_rz[:, 0:1], 0.5, None, ALU.mult)
            dve.tensor_scalar(b_zs[:], b_rz[:, 1:2], -0.5, None, ALU.mult)
            dve.tensor_scalar(eps1[:], eps_col[:], 1.0, None, ALU.add).then_inc(eps_ready, 1)
            dve.wait_ge(eps_ready, 1)
            dve.wait_ge(ident_ready, 1)
            dve.wait_ge(pads_ready, 1)
            for b in range(BP):
                for q in range(2):
                    ins = dve.tensor_scalar(diag[:, b, q, q, :], ident[:], eps1[:, 0:1], None, ALU.mult)
            ins.then_inc(setup_done, 1)
            dve.tensor_copy(gin1_hi[:], gin1[:]).then_inc(gin_hi_done, 1)
            dve.wait_ge(gin_hi_done, 1)
            dve.tensor_tensor(gin1_lo[:], gin1[:], gin1_hi[:].bitcast(F32), ALU.subtract).then_inc(gin_split, 1)

            def split_blocks(n, a, z):
                dve.tensor_copy(w_hi[:, a:z, :], w_t[:, a:z, :]).then_inc(w_hi_done, 1)
                dve.wait_ge(w_hi_done, n + 1)
                dve.tensor_tensor(w_lo[:, a:z, :], w_t[:, a:z, :], w_hi[:, a:z, :].bitcast(F32),
                                  ALU.subtract).then_inc(w_split, 1)

            dve.wait_ge(w_copied, 1)
            split_blocks(0, CONV1, GATE)

            def join_halves(i, st, mean, half, sq, var, eps_, sums, terms, done):
                dve.tensor_tensor(mean[:], st[:, :, 1], st[:, :, 4], ALU.add)
                dve.tensor_tensor(half[:], st[:, :, 1], st[:, :, 4], ALU.subtract)
                dve.tensor_tensor(var[:], st[:, :, 2], st[:, :, 5], ALU.add).then_inc(sums, 1)
                dve.wait_ge(sums, i)
                dve.tensor_tensor(sq[:], half[:], half[:], ALU.mult)
                dve.tensor_scalar(var[:], var[:], 1.0 / D, eps_, ALU.mult, ALU.add).then_inc(terms, 1)
                dve.wait_ge(terms, i)
                dve.scalar_tensor_tensor(var[:], sq[:], 0.25, var[:], ALU.mult, ALU.add).then_inc(done, 1)

            def iteration(i, b, previous, current, following):
                if current:
                    tiles = ps[:, CB:DB + 1:2, 0:2 * SW].rearrange("c k (t f) -> c k t f", t=2)
                    dve.wait_ge(msg_done, i + 1)
                    dve.tensor_tensor(s_nat[:].rearrange("c (k t) f -> c k t f", k=2), tiles[:, :, :, P:P + 3],
                                      bse_row[:].rearrange("c (k t) f -> c k t f", k=2), ALU.add)\
                        .then_inc(s_ready, 1)
                    dve.tensor_tensor(msg_pre[:].rearrange("c (k t) f -> c k t f", k=2), tiles[:, :, :, 0:P],
                                      bmsg_row[:].rearrange("c (k t) f -> c k t f", k=2), ALU.add)\
                        .then_inc(msg_added, 1)
                if previous:
                    dve.wait_ge(r_tanh, i)
                    dve.tensor_scalar(r[:], r_t[:], 0.5, 0.5, ALU.mult, ALU.add).then_inc(r_ready, 1)
                    dve.wait_ge(r_ready, i)
                    dve.scalar_tensor_tensor(u[:], ps[:, GNH, :], bhh[:, GATE_N:GATE_N + 1], r[:], ALU.add,
                                             ALU.mult).then_inc(u_ready, 1)
                    dve.wait_ge(n_done, i)
                    dve.wait_ge(u_ready, i)
                    dve.tensor_tensor(w[:], ps[:, GNI, :], u[:], ALU.add).then_inc(w_ready, 1)
                if current:
                    dve.wait_ge(sum_conv_done, i + 1)
                    x_v = xT[b][:].rearrange("c (b p m) -> c b p m", b=BP, p=2)
                    s_v = ps[:, CA, 0:BP * M].rearrange("c (b m) -> c b m", b=BP)
                    for p in range(2):
                        ins = dve.scalar_tensor_tensor(base[:, :, p, :], s_v, bn_shift[:, 1:2],
                                                       x_v[:, :, p, :], ALU.add, ALU.add)
                    ins.then_inc(base_ready, 1)
                    dve.wait_ge(lr_turned, i + 1)
                    dve.tensor_copy(right[:], ps[S_PAD:S_PAD + S_ROWS, DB, :]).then_inc(right_ready, 1)
                if previous:
                    dve.wait_ge(z_tanh, i)
                    dve.wait_ge(d_ready, i)
                    dve.scalar_tensor_tensor(e[:], z_t[:], 1.0, d[:], ALU.add, ALU.mult).then_inc(e_ready, 1)
                    dve.wait_ge(e_ready, i)
                    dve.scalar_tensor_tensor(yT[:], xT[1 - b][:], 4.0, e[:], ALU.mult, ALU.subtract)\
                        .then_inc(y_ready, 1)
                    dve.wait_ge(y_turned, i)
                    for t in range(TILES):
                        ins = dve.bn_stats(st1[:, t, :], ps[:, GR, t * P:(t + 1) * P])
                    ins.then_inc(ln1_stats, 1)
                    dve.wait_ge(ln1_stats, i)
                    join_halves(i, st1, mean1, half1, sq1, var1, 4 * LN_EPS, ln1_sums, ln1_terms, ln1_var)
                if current:
                    dve.wait_ge(adj_turned, i + 1)
                    dve.tensor_tensor(amask[:], ps[:, DA:DB + 1, :], expd[:], ALU.mult).then_inc(amask_ready, 1)
                if previous:
                    dve.wait_ge(ln1_rstd, i)
                    dve.scalar_tensor_tensor(shift1[:], mean1[:], -0.5, rstd1[:], ALU.mult, ALU.mult)\
                        .then_inc(ln1_shift, 1)
                if current:
                    dve.tensor_tensor(adjT[b][:], ps[:, DA:DB + 1, :],
                                      diag[:].rearrange("c b q p m -> c b (q p m)"), ALU.add)\
                        .then_inc(adjT_ready, 1)
                    dve.wait_ge(conv2_done, i + 1)
                    dve.wait_ge(base_ready, i + 1)
                    dve.tensor_tensor(conv_x[:], ps[:, CB, :], base[:].rearrange("c b p m -> c (b p m)"),
                                      ALU.add).then_inc(conv_added, 1)
                    dve.wait_ge(xc_hi_ready, i + 1)
                    dve.scalar_tensor_tensor(xc_lo[:], conv_x[:], 0.0, xc_hi[:].bitcast(F32), ALU.max,
                                             ALU.subtract).then_inc(xc_ready, 1)
                    dve.wait_ge(xn_hi_ready, i + 1)
                    dve.tensor_tensor(xn_lo[:], ps[:, GNI, :], xn_hi[:].bitcast(F32), ALU.subtract)\
                        .then_inc(xn_ready, 1)
                if previous:
                    dve.wait_ge(h_hi_ready, i)
                    dve.tensor_tensor(h_lo[:], ps[:, GNH, :], h_hi[:].bitcast(F32), ALU.subtract)\
                        .then_inc(h_ready, 1)
                if following:
                    dve.wait_ge(xT_ready, i + 2)
                    dve.tensor_copy(x_hi[:], xT[1 - b][:]).then_inc(x_hi_ready, 1)
                    dve.wait_ge(x_hi_ready, i + 2)
                    dve.tensor_tensor(x_lo[:], xT[1 - b][:], x_hi[:].bitcast(F32), ALU.subtract)\
                        .then_inc(x_ready, 1)
                if previous:
                    dve.wait_ge(gin_done, i)
                    dve.wait_ge(x1b_ready, i)
                    dve.tensor_tensor(y2[:], ps[:, DA, :].rearrange("c (t f) -> c t f", t=TILES), x1b[:], ALU.add)\
                        .then_inc(y2_ready, 1)
                    dve.wait_ge(y2_ready, i)
                    for t in range(TILES):
                        ins = dve.bn_stats(st2[:, t, :], y2[:, t, :])
                    ins.then_inc(ln2_stats, 1)
                    dve.wait_ge(ln2_stats, i)
                    join_halves(i, st2, mean2, half2, sq2, var2, LN_EPS, ln2_sums, ln2_terms, ln2_var)
                if following:
                    dve.wait_ge(h1_ready, i + 2)
                    dve.tensor_copy(hs_hi[:, 0], hs[:, 1]).then_inc(u1_hi_ready, 1)
                    dve.wait_ge(u1_hi_ready, i + 2)
                    dve.tensor_tensor(hs_lo[:, 0], hs[:, 1], hs_hi[:, 0].bitcast(F32), ALU.subtract)\
                        .then_inc(u1_ready, 1)
                    dve.tensor_tensor(hs[:, 2], hs[:, 0], hs[:, 1], ALU.subtract)
                    dve.tensor_tensor(hs[:, 3, :, 0:MP - 1], hs[:, 0, :, 1:MP], hs[:, 1, :, 0:MP - 1],
                                      ALU.subtract).then_inc(diffs_ready, 1)
                if previous:
                    dve.wait_ge(ln2_rstd, i)
                    dve.scalar_tensor_tensor(shift2[:], mean2[:], -0.5, rstd2[:], ALU.mult, ALU.mult)\
                        .then_inc(ln2_shift, 1)
                if following:
                    dve.wait_ge(diffs_ready, i + 2)
                    dve.tensor_copy(hs_hi[:, 1:3], hs[:, 2:4]).then_inc(diff_hi_ready, 1)
                    dve.wait_ge(diff_hi_ready, i + 2)
                    dve.tensor_tensor(hs_lo[:, 1:3], hs[:, 2:4], hs_hi[:, 1:3].bitcast(F32), ALU.subtract)\
                        .then_inc(diff_ready, 1)

            iteration(-1, 1, False, False, True)
            dve.wait_ge(w_copied, 7)
            taps = w_t[:, TAP:TAP + 2 * ODD, :].rearrange("c (a k) o -> c a k o", k=2)
            dve.tensor_tensor(w_t[:, SUM:BLOCKS, :], taps[:, :, 0, :], taps[:, :, 1, :], ALU.add)\
                .then_inc(w_summed, 1)
            dve.wait_ge(w_summed, 1)
            split_blocks(1, SUM, BLOCKS)
            split_blocks(2, TAP, SUM)
            split_blocks(3, GATE, TAP)
            iteration(0, 0, False, True, True)
            with dve.Fori(1, PAIRS - 2, 2) as t:
                iteration(t, 1, True, True, True)
                iteration(t + 1, 0, True, True, True)
            iteration(PAIRS - 1, 1, True, True, False)
            iteration(PAIRS, 0, True, False, False)

        @block.tensor
        def _(pe):
            pe.wait_ge(ident_ready, 1)
            pe.wait_ge(weights_loaded, 16 * N_BIG)
            pe.wait_ge(conv1_scaled, 1)
            natural = [conv1_nat[:]]
            for source in range(3):
                for g in range(3):
                    natural.append(hh_nat[:, g, :] if source == FROM_X else ih_nat[:, g, source * D:(source + 1) * D])
            natural += [conv2_nat[:, :, k] for k in range(TAPS)] + [msg_nat[:]]
            for k, block_ in enumerate(natural):
                if k == TAP:
                    pe.wait_ge(conv2_scaled, 1)
                ins = pe.transpose(ps[:, k // 4, (k % 4) * P:(k % 4 + 1) * P], block_, ident[:])
                if k % 4 == 3:
                    ins.then_inc(w_turned, 1)
            pe.transpose(ps[:, 7, 0:3], se_nat[:], ident[0:3, 0:3]).then_inc(w_turned, 1)

            def split_product(dst, block_, moving_hi, moving_lo, start, stop):
                pe.matmul(dst, w_hi[:, block_, :], moving_hi, start=start, stop=False)
                pe.matmul(dst, w_hi[:, block_, :], moving_lo, start=False, stop=False)
                return pe.matmul(dst, w_lo[:, block_, :], moving_hi, start=False, stop=stop)

            def parity_conv(dst, blocks, part, first, end):
                for a in range(first, end):
                    ins = split_product(dst, blocks[a], hs_hi[:, part, :, a:a + M], hs_lo[:, part, :, a:a + M],
                                        a == 0, a == len(blocks) - 1)
                return ins

            sum_taps = [SUM + a for a in range(ODD)] + [TAP + TAPS - 1]
            even_taps = [TAP + 2 * a for a in range(EVEN)]
            odd_taps = [TAP + 2 * a + 1 for a in range(ODD)]

            def iteration(i, b, previous, current, following):
                cb = ps[:, CB, :].rearrange("c (b p m) -> c b p m", b=BP, p=2)
                if current:
                    if not previous:
                        pe.wait_ge(w_split, 2)
                    pe.wait_ge(u1_ready, i + 1)
                    ca = ps[:, CA, 0:BP * M].rearrange("c (b m) -> c b m", b=BP)
                    parity_conv(ca, sum_taps, 0, 0, ODD)
                    if not previous:
                        pe.wait_ge(w_split, 3)
                    parity_conv(ca, sum_taps, 0, ODD, EVEN).then_inc(sum_conv_done, 1)
                    pe.wait_ge(lr_built, i + 1)
                    pe.wait_ge(msg_added, i + 1)
                    for t in range(TILES):
                        ins = pe.transpose(ps[:, DB, t * P:(t + 1) * P], lr[:, t, :].bitcast(F32), ident[:])
                    ins.then_inc(lr_turned, 1)
                    pe.wait_ge(diff_ready, i + 1)
                    parity_conv(cb[:, :, 0, :], even_taps, 1, 0, 5)
                    pe.wait_ge(left_ready, i + 1)
                    pe.wait_ge(right_ready, i + 1)
                    for k in range(BP):
                        for q in range(2):
                            m0 = (2 * k + q) * P
                            ins = pe.matmul(ps[:, DA + k, q * N:(q + 1) * N], left[:, m0:m0 + P],
                                            right[:, k * N:(k + 1) * N], start=True, stop=True)
                    ins.then_inc(dist_done, 1)
                    parity_conv(cb[:, :, 0, :], even_taps, 1, 5, EVEN)
                if previous:
                    pe.wait_ge(y_ready, i)
                    for t in range(TILES):
                        ins = pe.transpose(ps[:, GR, t * P:(t + 1) * P], yT[:, t * P:(t + 1) * P], ident[:])
                    ins.then_inc(y_turned, 1)
                if current:
                    pe.wait_ge(adj_loaded, 16 * (i + 1))
                    pe.wait_ge(exp_ready, i + 1)
                    for k in range(BP):
                        for q in range(2):
                            for p in range(2):
                                c0 = (2 * q + p) * P
                                ins = pe.transpose(ps[:, DA + k, c0:c0 + P], adj_nat[:, k, p, q::2], ident[:])
                    ins.then_inc(adj_turned, 1)
                    parity_conv(cb[:, :, 1, :], odd_taps, 2, 0, ODD).then_inc(conv2_done, 1)
                    pe.wait_ge(msg_ready, i + 1)
                    pe.wait_ge(amask_ready, i + 1)
                    for k in range(BP):
                        for q in range(2):
                            ins = pe.matmul(ps[:, GNI, k * N:(k + 1) * N], msg[:, 2 * k + q, :],
                                            amask[:, k, q * N:(q + 1) * N], start=(q == 0), stop=(q == 1))
                    ins.then_inc(xn_done, 1)
                if previous:
                    pe.wait_ge(x1_ready, i)
                    for k in range(BP):
                        for q in range(2):
                            ins = pe.matmul(ps[:, GNH, k * N:(k + 1) * N], x1[:, 2 * k + q, :],
                                            adjT[1 - b][:, k, q * N:(q + 1) * N], start=(q == 0), stop=(q == 1))
                    ins.then_inc(agg_done, 1)
                if current:
                    if not previous:
                        pe.wait_ge(w_split, 4)
                    split_product(ps[:, GR, :], GATE + 3 * FROM_X + GATE_R, x_hi[:], x_lo[:], True, False)
                    split_product(ps[:, GZ, :], GATE + 3 * FROM_X + GATE_Z, x_hi[:], x_lo[:], True, False)
                if previous:
                    pe.wait_ge(h_ready, i)
                if current:
                    split_product(ps[:, GNH, :], GATE + 3 * FROM_X + GATE_N, x_hi[:], x_lo[:], True, True)
                    pe.wait_ge(adjT_ready, i + 1)
                if previous:
                    for h, done in ((0, hidden0_done), (1, hidden1_done)):
                        cols = slice(h * P, (h + 1) * P)
                        pe.matmul(ps[:, DA + h, :], gin1_hi[:, cols], h_hi[:], start=True, stop=False)
                        pe.matmul(ps[:, DA + h, :], gin1_hi[:, cols], h_lo[:], start=False, stop=False)
                        pe.matmul(ps[:, DA + h, :], gin1_lo[:, cols], h_hi[:], start=False, stop=True)\
                            .then_inc(done, 1)
                if following:
                    pe.wait_ge(x_loaded, 16 * (i + 2))
                    if current:
                        pe.wait_ge(base_ready, i + 1)
                    else:
                        pe.wait_ge(w_copied, 8)
                    for t in range(TILES):
                        ins = pe.transpose(ps[:, CA, t * P:(t + 1) * P], x_nat[:, t // 2, t % 2, :], ident[:])
                    ins.then_inc(x_turned, 1)
                if current:
                    pe.wait_ge(xn_ready, i + 1)
                    split_product(ps[:, GR, :], GATE + 3 * FROM_NMP + GATE_R, xn_hi[:], xn_lo[:], False, False)
                    split_product(ps[:, GZ, :], GATE + 3 * FROM_NMP + GATE_Z, xn_hi[:], xn_lo[:], False, False)
                    split_product(ps[:, GNI, :], GATE + 3 * FROM_NMP + GATE_N, xn_hi[:], xn_lo[:], True, False)
                if previous:
                    pe.wait_ge(hidden_ready, i)
                    for t in range(TILES):
                        for h in range(2):
                            ins = pe.matmul(ps[:, DA, t * P:(t + 1) * P], hidden[:, h, t * P:(t + 1) * P],
                                            gin2[:, h, :], start=(h == 0), stop=(h == 1))
                    ins.then_inc(gin_done, 1)
                if following:
                    if not current:
                        pe.wait_ge(w_split, 1)
                    pe.wait_ge(x_ready, i + 2)
                    split_product(ps[:, CA, :], CONV1, x_hi[:], x_lo[:], True, True).then_inc(conv1_done, 1)
                if current:
                    pe.wait_ge(xc_ready, i + 1)
                    for g, bank, done in ((GATE_R, GR, r_done), (GATE_N, GNI, n_done), (GATE_Z, GZ, z_done)):
                        split_product(ps[:, bank, :], GATE + 3 * FROM_CONV + g, xc_hi[:], xc_lo[:], False, True)\
                            .then_inc(done, 1)
                if following:
                    for t in range(TILES):
                        bank, c0 = (CB, DB)[t // 2], (t % 2) * SW
                        ins = pe.matmul(ps[:, bank, c0:c0 + SW], xT[1 - b][:, t * P:(t + 1) * P], msgse[:],
                                        start=True, stop=True)
                    ins.then_inc(msg_done, 1)

            iteration(-1, 1, False, False, True)
            iteration(0, 0, False, True, True)
            pe.wait_ge(gin_split, 1)
            with pe.Fori(1, PAIRS - 2, 2) as t:
                iteration(t, 1, True, True, True)
                iteration(t + 1, 0, True, True, True)
            iteration(PAIRS - 1, 1, True, True, False)
            iteration(PAIRS, 0, True, False, False)


_INS = ['x', 'adj', 'L0_gnn_w_se', 'L0_gnn_b_se', 'L0_gnn_conv1_w', 'L0_gnn_bn1_g', 'L0_gnn_bn1_b', 'L0_gnn_bn1_m',
        'L0_gnn_bn1_v', 'L0_gnn_conv2_w', 'L0_gnn_bn2_g', 'L0_gnn_bn2_b', 'L0_gnn_bn2_m', 'L0_gnn_bn2_v',
        'L0_gnn_w_msg', 'L0_gnn_b_msg', 'L0_gnn_w_ih', 'L0_gnn_b_ih', 'L0_gnn_w_hh', 'L0_gnn_b_hh',
        'L1_gnn_eps', 'L1_gnn_W1', 'L1_gnn_b1', 'L1_gnn_W2', 'L1_gnn_b2']


def kernel(**inputs):
    import numpy as _np
    import concourse.bacc as _bacc
    from concourse import mybir as _mybir
    from concourse.bass_utils import run_bass_kernel_spmd as _run

    nc = _bacc.Bacc("TRN2", target_bir_lowering=False, num_devices=1)
    arrays, args = {}, []
    for name in _INS:
        a = _np.ascontiguousarray(inputs[name])
        arrays[f"in_{name}_dram"] = a
        args.append(nc.dram_tensor(f"in_{name}_dram", a.shape, _mybir.dt.from_np(a.dtype), kind="ExternalInput").ap())
    shape = tuple(inputs['x'].shape)
    args.append(nc.dram_tensor("out_0_dram", shape, _mybir.dt.float32, kind="ExternalOutput").ap())
    build_program(nc, *args)
    r = _run(nc, [arrays], core_ids=[0])
    return r.results[0]["out_0_dram"]
```

```python
import concourse.bass as bass
from concourse import mybir
from contextlib import ExitStack

F32 = mybir.dt.float32
F32R = mybir.dt.float32r
ALU = mybir.AluOpType
ACT = mybir.ActivationFunctionType

BN_EPS = 1e-5
LN_EPS = 1e-5


def build_program(nc, x, adj, w_se, b_se, conv1_w, bn1_g, bn1_b, bn1_m, bn1_v, conv2_w, bn2_g, bn2_b, bn2_m,
                  bn2_v, w_msg, b_msg, w_ih, b_ih, w_hh, b_hh, eps, W1, b1, W2, b2, out):
    B, N, D = x.shape
    HID = W1.shape[1]
    TAPS = conv2_w.shape[2]
    P = 128
    BP = 2
    PAIRS = B // BP
    M = N // 2
    T = BP * N
    TILES = T // P
    PAD = TAPS // 4
    MP = M + 2 * PAD
    EVEN, ODD = (TAPS + 1) // 2, TAPS // 2
    assert D == P and M == P and HID == 2 * P and TAPS == 17 and PAIRS % 2 == 0 and PAIRS >= 4

    SUM = 0
    TAP = SUM + ODD
    GATE = TAP + TAPS
    BLOCKS = GATE + 9
    FROM_CONV, FROM_NMP, FROM_X = range(3)
    GATE_R, GATE_Z, GATE_N = range(3)
    S_ROWS = 24
    S_PAD = 32
    SW = P + 4

    x_pairs = x.rearrange("(i b) (m p) d -> i m b p d", b=BP, p=2)
    adj_pairs = adj.rearrange("(i b) (m p) c -> i m b p c", b=BP, p=2)
    out_pairs = out.rearrange("(i b) (m p) d -> i m b p d", b=BP, p=2)

    with ExitStack() as ctx:
        def sb(name, shape, dt=F32):
            return ctx.enter_context(nc.sbuf_tensor(name, shape, dt))

        def sem(name):
            return ctx.enter_context(nc.semaphore(name))

        ps = ctx.enter_context(nc.psum_tensor("ps", [P, 8, 512], F32))
        CA, CB, DA, DB, GR, GNH, GNI, GZ = range(8)

        ident = sb("ident", [P, P])
        conv1_nat = sb("conv1_nat", [P, D])
        conv2_nat = sb("conv2_nat", [P, D, TAPS])
        ih_nat = sb("ih_nat", [P, 3, 2 * D])
        hh_nat = sb("hh_nat", [P, 3, D])
        msg_nat = sb("msg_nat", [P, D])
        se_nat = sb("se_nat", [3, D])
        sums_nat = sb("sums_nat", [P, D, ODD])
        conv1_hi = sb("conv1_hi", [P, P], F32R)
        conv1_lo = sb("conv1_lo", [P, P], F32R)
        w_hi = sb("w_hi", [P, BLOCKS, P], F32R)
        w_lo = sb("w_lo", [P, BLOCKS, P], F32R)
        msgse = sb("msgse", [P, SW])
        gin1 = sb("gin1", [P, HID])
        gin1_hi = sb("gin1_hi", [P, HID], F32R)
        gin1_lo = sb("gin1_lo", [P, HID], F32R)
        gin2 = sb("gin2", [P, 2, D])
        bn = sb("bn", [P, 2, 4])
        bn_r = sb("bn_r", [P, 2])
        bn_scale = sb("bn_scale", [P, 2])
        bn_shift = sb("bn_shift", [P, 2])
        bn_t = sb("bn_t", [P, 2])
        bih = sb("bih", [P, 3])
        bhh = sb("bhh", [P, 3])
        b_rz = sb("b_rz", [P, 2])
        b_rs = sb("b_rs", [P, 1])
        b_zs = sb("b_zs", [P, 1])
        b1_col = sb("b1_col", [P, 2])
        eps_col = sb("eps_col", [P, 1])
        eps1 = sb("eps1", [P, 1])
        bmsg_row = sb("bmsg_row", [P, D])
        bse_row = sb("bse_row", [P, 3])
        b2_row = sb("b2_row", [P, D])
        diag = sb("diag", [P, BP, 2, 2, P])
        minus_half = sb("minus_half", [P, TILES])
        zeros = sb("zeros", [P, TILES, 6])

        x_nat = sb("x_nat", [P, BP, 2, D])
        adj_nat = sb("adj_nat", [P, BP, 2, N])
        xT = [sb(f"xT{k}", [P, T]) for k in range(2)]
        x_hi = sb("x_hi", [P, T], F32R)
        x_lo = sb("x_lo", [P, T], F32R)
        hs = sb("hs", [P, 4, BP, MP])
        hs_hi = sb("hs_hi", [P, 3, BP, MP], F32R)
        hs_lo = sb("hs_lo", [P, 3, BP, MP], F32R)
        msg_pre = sb("msg_pre", [P, TILES, D])
        msg = sb("msg", [P, TILES, D])
        s_nat = sb("s_nat", [P, TILES, 3])
        s_sq = sb("s_sq", [P, TILES, 3])
        lr = sb("lr", [P, TILES, P], F32R)
        left = sb("left", [S_ROWS, T], F32R)
        right = sb("right", [S_ROWS, T], F32R)
        expd = sb("expd", [P, BP, 512])
        amask = sb("amask", [P, BP, 512])
        adjT = [sb(f"adjT{k}", [P, BP, 512]) for k in range(2)]
        base = sb("base", [P, BP, 2, M])
        conv_x = sb("conv_x", [P, T])
        xc_hi = sb("xc_hi", [P, T], F32R)
        xc_lo = sb("xc_lo", [P, T], F32R)
        xn_hi = sb("xn_hi", [P, T], F32R)
        xn_lo = sb("xn_lo", [P, T], F32R)
        r_t = sb("r_t", [P, T])
        z_t = sb("z_t", [P, T])
        r = sb("r", [P, T])
        u = sb("u", [P, T])
        w = sb("w", [P, T])
        n_t = sb("n_t", [P, T])
        d = sb("d", [P, T])
        e = sb("e", [P, T])
        yT = sb("yT", [P, T])
        st1 = sb("st1", [P, TILES, 6])
        mean1 = sb("mean1", [P, TILES])
        half1 = sb("half1", [P, TILES])
        sq1 = sb("sq1", [P, TILES])
        var1 = sb("var1", [P, TILES])
        rstd1 = sb("rstd1", [P, TILES])
        shift1 = sb("shift1", [P, TILES])
        neg_mean1 = sb("neg_mean1", [P, TILES])
        x1 = sb("x1", [P, TILES, D])
        x1b = sb("x1b", [P, TILES, D])
        h_hi = sb("h_hi", [P, T], F32R)
        h_lo = sb("h_lo", [P, T], F32R)
        hidden = sb("hidden", [P, 2, T])
        y2 = sb("y2", [P, TILES, D])
        st2 = sb("st2", [P, TILES, 6])
        mean2 = sb("mean2", [P, TILES])
        half2 = sb("half2", [P, TILES])
        sq2 = sb("sq2", [P, TILES])
        var2 = sb("var2", [P, TILES])
        rstd2 = sb("rstd2", [P, TILES])
        shift2 = sb("shift2", [P, TILES])
        neg_mean2 = sb("neg_mean2", [P, TILES])
        out_nat = sb("out_nat", [P, TILES, D])

        ident_zero = sem("ident_zero")
        ident_ready = sem("ident_ready")
        weights_loaded = sem("weights_loaded")
        small_loaded = sem("small_loaded")
        consts_ready = sem("consts_ready")
        pads_ready = sem("pads_ready")
        bn_loaded = sem("bn_loaded")
        conv1_loaded = sem("conv1_loaded")
        conv2_loaded = sem("conv2_loaded")
        bn_rsqrt = sem("bn_rsqrt")
        bn_scaled = sem("bn_scaled")
        bn_mean = sem("bn_mean")
        bn_var = sem("bn_var")
        eps_ready = sem("eps_ready")
        bias_summed = sem("bias_summed")
        taps_summed = sem("taps_summed")
        conv2_scaled = sem("conv2_scaled")
        first_turned = sem("first_turned")
        conv1_hi_ready = sem("conv1_hi_ready")
        conv1_split = sem("conv1_split")
        msgse_ready = sem("msgse_ready")
        w_turned = sem("w_turned")
        w_hi_ready = sem("w_hi_ready")
        w_split = sem("w_split")
        gin_hi_ready = sem("gin_hi_ready")
        gin_split = sem("gin_split")
        setup_done = sem("setup_done")

        x_loaded = sem("x_loaded")
        adj_loaded = sem("adj_loaded")
        out_free = sem("out_free")
        x_turned = sem("x_turned")
        conv1_done = sem("conv1_done")
        msg_done = sem("msg_done")
        lr_turned = sem("lr_turned")
        sum_conv_done = sem("sum_conv_done")
        dist_done = sem("dist_done")
        adj_turned = sem("adj_turned")
        y_turned = sem("y_turned")
        conv2_done = sem("conv2_done")
        xn_done = sem("xn_done")
        agg_done = sem("agg_done")
        r_done = sem("r_done")
        z_done = sem("z_done")
        n_done = sem("n_done")
        hidden0_done = sem("hidden0_done")
        hidden1_done = sem("hidden1_done")
        gin_done = sem("gin_done")
        r_tanh = sem("r_tanh")
        z_tanh = sem("z_tanh")
        msg_ready = sem("msg_ready")
        n_ready = sem("n_ready")
        rows_ready = sem("rows_ready")
        exp_ready = sem("exp_ready")
        x1_ready = sem("x1_ready")
        xc_hi_ready = sem("xc_hi_ready")
        xn_hi_ready = sem("xn_hi_ready")
        h_hi_ready = sem("h_hi_ready")
        hidden_ready = sem("hidden_ready")
        xT_ready = sem("xT_ready")
        h1_ready = sem("h1_ready")
        out_ready = sem("out_ready")
        s_ready = sem("s_ready")
        msg_added = sem("msg_added")
        u_ready = sem("u_ready")
        w_ready = sem("w_ready")
        base_ready = sem("base_ready")
        e_ready = sem("e_ready")
        y_ready = sem("y_ready")
        ln1_stats = sem("ln1_stats")
        ln1_sums = sem("ln1_sums")
        ln1_terms = sem("ln1_terms")
        ln1_var = sem("ln1_var")
        amask_ready = sem("amask_ready")
        adjT_ready = sem("adjT_ready")
        conv_added = sem("conv_added")
        xc_ready = sem("xc_ready")
        xn_ready = sem("xn_ready")
        h_ready = sem("h_ready")
        x_hi_ready = sem("x_hi_ready")
        x_ready = sem("x_ready")
        u1_hi_ready = sem("u1_hi_ready")
        u1_ready = sem("u1_ready")
        diffs_ready = sem("diffs_ready")
        diff_hi_ready = sem("diff_hi_ready")
        diff_ready = sem("diff_ready")
        y2_ready = sem("y2_ready")
        ln2_stats = sem("ln2_stats")
        ln2_sums = sem("ln2_sums")
        ln2_terms = sem("ln2_terms")
        ln2_var = sem("ln2_var")
        s_hi_ready = sem("s_hi_ready")
        s_lo_ready = sem("s_lo_ready")
        lr_built = sem("lr_built")
        r_ready = sem("r_ready")
        d_ready = sem("d_ready")
        ln1_rstd = sem("ln1_rstd")
        ln1_shift = sem("ln1_shift")
        x1b_ready = sem("x1b_ready")
        ln2_rstd = sem("ln2_rstd")
        ln2_shift = sem("ln2_shift")

        N_BIG, N_SMALL = 6, 3 + 3 + 2 + 1 + 3

        block = ctx.enter_context(nc.Block())

        @block.sync
        def _(sp):
            def columns(dst, src, loaded):
                for k in range(src.shape[0] // P):
                    sp.dma_start(dst[:, k:k + 1], src[k * P:(k + 1) * P].unsqueeze(1)).then_inc(loaded, 16)

            sp.dma_start(x_nat[:], x_pairs[0]).then_inc(x_loaded, 16)
            sp.dma_start(conv1_nat[:], conv1_w.rearrange("o i k -> o (i k)")).then_inc(conv1_loaded, 16)
            for which, group in enumerate(((bn1_g, bn1_b, bn1_m, bn1_v), (bn2_g, bn2_b, bn2_m, bn2_v))):
                for k, vector in enumerate(group):
                    columns(bn[:, which, k:k + 1], vector, bn_loaded)
            sp.dma_start(ih_nat[:], w_ih.rearrange("(g o) i -> o g i", g=3)).then_inc(weights_loaded, 16)
            sp.dma_start(adj_nat[:], adj_pairs[0]).then_inc(adj_loaded, 16)
            columns(bih, b_ih, small_loaded)
            columns(bhh, b_hh, small_loaded)
            columns(b1_col, b1, small_loaded)
            sp.dma_start(gin1[:], W1).then_inc(weights_loaded, 16)
            sp.dma_start(gin2[:], W2.rearrange("(h p) d -> p h d", h=2)).then_inc(weights_loaded, 16)

            def iteration(i, previous, current, following):
                if current and following:
                    sp.wait_ge(x_turned, i + 1)
                    sp.dma_start(x_nat[:], x_pairs[i + 1]).then_inc(x_loaded, 16)
                    sp.wait_ge(adj_turned, i + 1)
                    sp.dma_start(adj_nat[:], adj_pairs[i + 1]).then_inc(adj_loaded, 16)
                if previous:
                    sp.wait_ge(out_ready, i)
                    sp.dma_start(out_pairs[i - 1], out_nat[:].rearrange("p (b q) d -> p b q d", b=BP))\
                        .then_inc(out_free, 16)

            iteration(0, False, True, True)
            with sp.Fori(1, PAIRS - 2, 2) as t:
                iteration(t, True, True, True)
                iteration(t + 1, True, True, True)
            iteration(PAIRS - 1, True, True, False)
            iteration(PAIRS, True, False, False)
            sp.wait_ge(out_free, 16 * (PAIRS + 1))

        @block.gpsimd
        def _(pool):
            pool.memset(ident[:], 0.0).then_inc(ident_zero, 1)
            pool.memset(out_nat[:, 0, 0:1], 0.0).then_inc(out_free, 16)
            pool.wait_ge(ident_zero, 1)
            pool.affine_select(out=ident[:], in_=ident[:], compare_op=ALU.not_equal, fill=1.0, base=0,
                               pattern=[[-1, P]], channel_multiplier=1).then_inc(ident_ready, 1)
            pool.memset(zeros[:], 0.0)
            pool.memset(minus_half[:], -0.5).then_inc(consts_ready, 1)
            pool.memset(lr[:].bitcast(F32), 0.0).then_inc(consts_ready, 1)
            pool.wait_ge(consts_ready, 2)
            pool.memset(lr[:, :, 18:24].bitcast(F32), 1.0).then_inc(consts_ready, 1)
            pool.memset(lr[:, :, S_PAD + 12:S_PAD + 18].bitcast(F32), 1.0).then_inc(consts_ready, 1)
            pool.wait_ge(consts_ready, 4)
            pool.wait_ge(bn_var, 1)
            pool.tensor_tensor(bn_r[:], bn_t[:], minus_half[:, 0:2], ALU.pow).then_inc(bn_rsqrt, 1)
            pool.wait_ge(weights_loaded, 16 * N_BIG)
            pool.tensor_copy(gin1_hi[:], gin1[:]).then_inc(gin_hi_ready, 1)
            pool.wait_ge(gin_hi_ready, 1)
            pool.tensor_tensor(gin1_lo[:], gin1[:], gin1_hi[:].bitcast(F32), ALU.subtract).then_inc(gin_split, 1)

            def build_lr(n):
                hi, lo = lr[:, :, 0:3], lr[:, :, 6:9]
                pool.wait_ge(s_ready, n)
                pool.tensor_tensor(s_sq[:], s_nat[:], s_nat[:], ALU.mult)
                pool.tensor_tensor(lr[:, :, 12:15], s_nat[:], s_nat[:], ALU.mult)
                pool.tensor_copy(hi, s_nat[:]).then_inc(s_hi_ready, 1)
                pool.wait_ge(s_hi_ready, n)
                pool.tensor_tensor(lo, s_nat[:], hi.bitcast(F32), ALU.subtract)
                pool.tensor_tensor(lr[:, :, 15:18], s_sq[:], lr[:, :, 12:15].bitcast(F32),
                                   ALU.subtract).then_inc(s_lo_ready, 1)
                pool.tensor_copy(lr[:, :, 3:6], hi.bitcast(F32))
                for at in (0, 6):
                    pool.tensor_scalar(lr[:, :, S_PAD + at:S_PAD + at + 3], hi.bitcast(F32), -2.0, 0.0,
                                       ALU.mult, ALU.add)
                pool.wait_ge(s_lo_ready, n)
                pool.tensor_tensor(lr[:, :, S_PAD + 18:S_PAD + 24], lr[:, :, 12:18].bitcast(F32),
                                   zeros[:], ALU.add)
                pool.tensor_copy(lr[:, :, 9:12], lo.bitcast(F32))
                for at in (3, 9):
                    ins = pool.tensor_scalar(lr[:, :, S_PAD + at:S_PAD + at + 3], lo.bitcast(F32), -2.0, 0.0,
                                             ALU.mult, ALU.add)
                ins.then_inc(lr_built, 1)

            def iteration(i, b, previous, current, following):
                if previous:
                    pool.wait_ge(ln1_var, i)
                    pool.tensor_tensor(neg_mean1[:], mean1[:], minus_half[:], ALU.mult)
                    pool.tensor_tensor(rstd1[:], var1[:], minus_half[:], ALU.pow).then_inc(ln1_rstd, 1)
                    pool.wait_ge(ln1_rstd, i)
                    pool.tensor_tensor(shift1[:], neg_mean1[:], rstd1[:], ALU.mult).then_inc(ln1_shift, 1)
                    pool.wait_ge(x1_ready, i)
                    pool.tensor_tensor(x1b[:], x1[:], b2_row[:].unsqueeze(1).to_broadcast([P, TILES, D]),
                                       ALU.add).then_inc(x1b_ready, 1)
                if current:
                    pool.wait_ge(n_ready, i + 1)
                    pool.tensor_tensor(d[:], xT[b][:], n_t[:], ALU.subtract).then_inc(d_ready, 1)
                if following:
                    build_lr(i + 2)
                if previous:
                    pool.wait_ge(ln2_var, i)
                    pool.tensor_tensor(neg_mean2[:], mean2[:], minus_half[:], ALU.mult)
                    pool.tensor_tensor(rstd2[:], var2[:], minus_half[:], ALU.pow).then_inc(ln2_rstd, 1)
                    pool.wait_ge(ln2_rstd, i)
                    pool.tensor_tensor(shift2[:], neg_mean2[:], rstd2[:], ALU.mult).then_inc(ln2_shift, 1)

            pool.wait_ge(small_loaded, 16 * N_SMALL)
            iteration(-1, 1, False, False, True)
            iteration(0, 0, False, True, True)
            with pool.Fori(1, PAIRS - 2, 2) as t:
                iteration(t, 1, True, True, True)
                iteration(t + 1, 0, True, True, True)
            iteration(PAIRS - 1, 1, True, True, False)
            iteration(PAIRS, 0, True, False, False)

        WAVES = [(2, 0, 4), (3, 4, 4), (4, 8, 4), (5, 12, 4), (6, 16, 4), (7, 20, 4), (2, 24, 4), (4, 28, 4), (5, 32, 2)]
        TAPS_SPLIT, GATES_SPLIT = 7, len(WAVES)
        assert sum(n for _, _, n in WAVES) == BLOCKS

        @block.scalar
        def _(act):
            act.dma_start(conv2_nat[:], conv2_w).then_inc(conv2_loaded, 16)
            act.dma_start(msg_nat[:], w_msg).then_inc(weights_loaded, 16)
            act.dma_start(se_nat[:], w_se).then_inc(weights_loaded, 16)
            act.dma_start(bse_row[:], b_se.partition_broadcast(P)).then_inc(small_loaded, 16)
            act.dma_start(bmsg_row[:], b_msg.partition_broadcast(P)).then_inc(small_loaded, 16)
            act.dma_start(hh_nat[:], w_hh.rearrange("(g o) i -> o g i", g=3)).then_inc(weights_loaded, 16)
            act.dma_start(eps_col[:], eps.partition_broadcast(P)).then_inc(small_loaded, 16)
            act.dma_start(b2_row[:], b2.partition_broadcast(P)).then_inc(small_loaded, 16)

            def iteration(i, b, previous, current, following):
                if previous:
                    act.wait_ge(ln1_shift, i)
                    for t in range(TILES):
                        ins = act.activation(x1[:, t, :], ps[:, GR, t * P:(t + 1) * P], ACT.Identity,
                                             bias=shift1[:, t:t + 1], scale=rstd1[:, t:t + 1])
                    ins.then_inc(x1_ready, 1)
                if current:
                    act.wait_ge(conv_added, i + 1)
                    act.activation(xc_hi[:], conv_x[:], ACT.Relu).then_inc(xc_hi_ready, 1)
                if previous:
                    act.wait_ge(agg_done, i)
                    act.activation(h_hi[:], ps[:, CA, :], ACT.Copy).then_inc(h_hi_ready, 1)
                if current:
                    act.wait_ge(xn_done, i + 1)
                    act.activation(xn_hi[:], ps[:, GNI, :], ACT.Copy).then_inc(xn_hi_ready, 1)
                if previous:
                    act.wait_ge(hidden0_done, i)
                    act.activation(hidden[:, 0, :], ps[:, DA, :], ACT.Relu, bias=b1_col[:, 0:1])
                    act.wait_ge(hidden1_done, i)
                    act.activation(hidden[:, 1, :], ps[:, DB, :], ACT.Relu, bias=b1_col[:, 1:2])\
                        .then_inc(hidden_ready, 1)
                if following:
                    act.wait_ge(x_turned, i + 2)
                    act.activation(xT[1 - b][:], ps[:, CA, :], ACT.Copy).then_inc(xT_ready, 1)
                if current:
                    act.wait_ge(r_done, i + 1)
                    act.activation(r_t[:], ps[:, GR, :], ACT.Tanh, bias=b_rs[:], scale=0.5).then_inc(r_tanh, 1)
                    act.wait_ge(z_done, i + 1)
                    act.activation(z_t[:], ps[:, GZ, :], ACT.Tanh, bias=b_zs[:], scale=-0.5)\
                        .then_inc(z_tanh, 1)
                else:
                    if following:
                        act.wait_ge(setup_done, 1)
                if following:
                    act.wait_ge(conv1_done, i + 2)
                    for p in range(2):
                        ins = act.activation(hs[:, p, :, PAD:PAD + M],
                                             ps[:, CA, :].rearrange("c (b p m) -> c b p m", b=BP, p=2)[:, :, p, :],
                                             ACT.Relu, bias=bn_shift[:, 0:1], scale=bn_scale[:, 0:1])
                    ins.then_inc(h1_ready, 1)
                if current:
                    act.wait_ge(w_ready, i + 1)
                    act.activation(n_t[:], w[:], ACT.Tanh, bias=bih[:, GATE_N:GATE_N + 1]).then_inc(n_ready, 1)
                if following and not current:
                    for n, (bank, first, blocks) in enumerate(WAVES):
                        act.wait_ge(w_turned, n + 1)
                        act.activation(w_hi[:, first:first + blocks, :], ps[:, bank, 0:blocks * P], ACT.Copy)\
                            .then_inc(w_hi_ready, 1)
                if following:
                    act.wait_ge(msg_added, i + 2)
                    act.activation(msg[:], msg_pre[:], ACT.Relu).then_inc(msg_ready, 1)
                    act.wait_ge(lr_turned, i + 2)
                    act.activation(left[:], ps[0:S_ROWS, DB, :], ACT.Copy)
                    act.activation(right[:], ps[S_PAD:S_PAD + S_ROWS, DB, :], ACT.Copy).then_inc(rows_ready, 1)
                    act.wait_ge(dist_done, i + 2)
                    act.activation(expd[:], ps[:, DA:DB + 1, :], ACT.Exp, scale=-1.0).then_inc(exp_ready, 1)
                if previous:
                    act.wait_ge(ln2_shift, i)
                    act.wait_ge(out_free, 16 * i)
                    for t in range(TILES):
                        ins = act.activation(out_nat[:, t, :], y2[:, t, :], ACT.Identity,
                                             bias=shift2[:, t:t + 1], scale=rstd2[:, t:t + 1])
                    ins.then_inc(out_ready, 1)

            act.wait_ge(first_turned, 1)
            act.activation(conv1_hi[:], ps[:, CB, 0:P], ACT.Copy)
            act.activation(msgse[:, 0:P + 3], ps[:, CB, P:2 * P + 3], ACT.Copy).then_inc(msgse_ready, 1)
            iteration(-1, 1, False, False, True)
            iteration(0, 0, False, True, True)
            with act.Fori(1, PAIRS - 2, 2) as t:
                iteration(t, 1, True, True, True)
                iteration(t + 1, 0, True, True, True)
            iteration(PAIRS - 1, 1, True, True, False)
            iteration(PAIRS, 0, True, False, False)

        @block.vector
        def _(dve):
            dve.memset(hs[:], 0.0)
            dve.memset(msgse[:, P + 3:SW], 0.0)
            dve.memset(diag[:], 0.0).then_inc(pads_ready, 1)
            dve.wait_ge(conv2_loaded, 16)
            dve.tensor_tensor(sums_nat[:], conv2_nat[:, :, 0:2 * ODD:2], conv2_nat[:, :, 1:2 * ODD:2], ALU.add)\
                .then_inc(taps_summed, 1)
            dve.wait_ge(bn_loaded, 16 * 8)
            dve.tensor_scalar(bn_t[:], bn[:, :, 3], BN_EPS, None, ALU.add).then_inc(bn_var, 1)
            dve.wait_ge(bn_rsqrt, 1)
            dve.tensor_tensor(bn_scale[:], bn[:, :, 0], bn_r[:], ALU.mult).then_inc(bn_scaled, 1)
            dve.wait_ge(bn_scaled, 1)
            dve.wait_ge(taps_summed, 1)
            dve.tensor_scalar(sums_nat[:], sums_nat[:], bn_scale[:, 1:2], None, ALU.mult)
            dve.tensor_scalar(conv2_nat[:], conv2_nat[:], bn_scale[:, 1:2], None, ALU.mult)\
                .then_inc(conv2_scaled, 1)
            dve.tensor_tensor(bn_t[:], bn[:, :, 2], bn_scale[:], ALU.mult).then_inc(bn_mean, 1)
            dve.wait_ge(small_loaded, 16 * N_SMALL)
            dve.tensor_tensor(b_rz[:], bih[:, 0:2], bhh[:, 0:2], ALU.add)
            dve.tensor_scalar(eps1[:], eps_col[:], 1.0, None, ALU.add).then_inc(bias_summed, 1)
            dve.wait_ge(bn_mean, 1)
            dve.tensor_tensor(bn_shift[:], bn[:, :, 1], bn_t[:], ALU.subtract)
            dve.wait_ge(bias_summed, 1)
            dve.tensor_scalar(b_rs[:], b_rz[:, 0:1], 0.5, None, ALU.mult)
            dve.tensor_scalar(b_zs[:], b_rz[:, 1:2], -0.5, None, ALU.mult).then_inc(setup_done, 1)
            dve.wait_ge(msgse_ready, 1)
            dve.tensor_tensor(conv1_lo[:], ps[:, CB, 0:P], conv1_hi[:].bitcast(F32), ALU.subtract)\
                .then_inc(conv1_split, 1)

            def join_halves(i, st, mean, half, sq, var, eps_, sums, terms, done):
                dve.tensor_tensor(mean[:], st[:, :, 1], st[:, :, 4], ALU.add)
                dve.tensor_tensor(half[:], st[:, :, 1], st[:, :, 4], ALU.subtract)
                dve.tensor_tensor(var[:], st[:, :, 2], st[:, :, 5], ALU.add).then_inc(sums, 1)
                dve.wait_ge(sums, i)
                dve.tensor_tensor(sq[:], half[:], half[:], ALU.mult)
                dve.tensor_scalar(var[:], var[:], 1.0 / D, eps_, ALU.mult, ALU.add).then_inc(terms, 1)
                dve.wait_ge(terms, i)
                dve.scalar_tensor_tensor(var[:], sq[:], 0.25, var[:], ALU.mult, ALU.add).then_inc(done, 1)

            def iteration(i, b, previous, current, following):
                if previous:
                    dve.wait_ge(y_turned, i)
                    for t in range(TILES):
                        ins = dve.bn_stats(st1[:, t, :], ps[:, GR, t * P:(t + 1) * P])
                    ins.then_inc(ln1_stats, 1)
                    dve.wait_ge(ln1_stats, i)
                    join_halves(i, st1, mean1, half1, sq1, var1, 4 * LN_EPS, ln1_sums, ln1_terms, ln1_var)
                if current:
                    dve.wait_ge(adj_turned, i + 1)
                    dve.tensor_tensor(amask[:], ps[:, DA:DB + 1, :], expd[:], ALU.mult).then_inc(amask_ready, 1)
                    dve.tensor_tensor(adjT[b][:], ps[:, DA:DB + 1, :],
                                      diag[:].rearrange("c b q p m -> c b (q p m)"), ALU.add)\
                        .then_inc(adjT_ready, 1)
                    dve.wait_ge(conv2_done, i + 1)
                    dve.tensor_tensor(conv_x[:], ps[:, CB, :], base[:].rearrange("c b p m -> c (b p m)"),
                                      ALU.add).then_inc(conv_added, 1)
                    dve.wait_ge(xc_hi_ready, i + 1)
                    dve.scalar_tensor_tensor(xc_lo[:], conv_x[:], 0.0, xc_hi[:].bitcast(F32), ALU.max,
                                             ALU.subtract).then_inc(xc_ready, 1)
                if previous:
                    dve.wait_ge(h_hi_ready, i)
                    dve.tensor_tensor(h_lo[:], ps[:, CA, :], h_hi[:].bitcast(F32), ALU.subtract)\
                        .then_inc(h_ready, 1)
                if current:
                    dve.wait_ge(xn_hi_ready, i + 1)
                    dve.tensor_tensor(xn_lo[:], ps[:, GNI, :], xn_hi[:].bitcast(F32), ALU.subtract)\
                        .then_inc(xn_ready, 1)
                if following:
                    dve.wait_ge(xT_ready, i + 2)
                    dve.tensor_copy(x_hi[:], xT[1 - b][:]).then_inc(x_hi_ready, 1)
                    dve.wait_ge(x_hi_ready, i + 2)
                    dve.tensor_tensor(x_lo[:], xT[1 - b][:], x_hi[:].bitcast(F32), ALU.subtract)\
                        .then_inc(x_ready, 1)
                if current:
                    dve.wait_ge(r_tanh, i + 1)
                    dve.tensor_scalar(r[:], r_t[:], 0.5, 0.5, ALU.mult, ALU.add).then_inc(r_ready, 1)
                    dve.wait_ge(r_ready, i + 1)
                    dve.scalar_tensor_tensor(u[:], ps[:, GNH, :], bhh[:, GATE_N:GATE_N + 1], r[:], ALU.add,
                                             ALU.mult).then_inc(u_ready, 1)
                    dve.wait_ge(n_done, i + 1)
                    dve.wait_ge(u_ready, i + 1)
                    dve.tensor_tensor(w[:], ps[:, GNI, :], u[:], ALU.add).then_inc(w_ready, 1)
                if following:
                    dve.wait_ge(h1_ready, i + 2)
                    dve.tensor_copy(hs_hi[:, 0], hs[:, 1]).then_inc(u1_hi_ready, 1)
                    dve.wait_ge(u1_hi_ready, i + 2)
                    dve.tensor_tensor(hs_lo[:, 0], hs[:, 1], hs_hi[:, 0].bitcast(F32), ALU.subtract)\
                        .then_inc(u1_ready, 1)
                    if not current:
                        for n in range(2):
                            split_wave(n)
                    dve.tensor_tensor(hs[:, 2], hs[:, 0], hs[:, 1], ALU.subtract)
                    dve.tensor_tensor(hs[:, 3, :, 0:MP - 1], hs[:, 0, :, 1:MP], hs[:, 1, :, 0:MP - 1],
                                      ALU.subtract).then_inc(diffs_ready, 1)
                    tiles = ps[:, CB:DB + 1:2, 0:2 * SW].rearrange("c k (t f) -> c k t f", t=2)
                    dve.wait_ge(msg_done, i + 2)
                    dve.tensor_tensor(s_nat[:].rearrange("c (k t) f -> c k t f", k=2), tiles[:, :, :, P:P + 3],
                                      bse_row[:].unsqueeze(1).unsqueeze(1).to_broadcast([P, 2, 2, 3]), ALU.add)\
                        .then_inc(s_ready, 1)
                    dve.wait_ge(diffs_ready, i + 2)
                    dve.tensor_copy(hs_hi[:, 1:3], hs[:, 2:4]).then_inc(diff_hi_ready, 1)
                    dve.wait_ge(diff_hi_ready, i + 2)
                    dve.tensor_tensor(hs_lo[:, 1:3], hs[:, 2:4], hs_hi[:, 1:3].bitcast(F32), ALU.subtract)\
                        .then_inc(diff_ready, 1)
                    dve.tensor_tensor(msg_pre[:].rearrange("c (k t) f -> c k t f", k=2), tiles[:, :, :, 0:P],
                                      bmsg_row[:].unsqueeze(1).unsqueeze(1).to_broadcast([P, 2, 2, D]), ALU.add)\
                        .then_inc(msg_added, 1)
                if current:
                    dve.wait_ge(z_tanh, i + 1)
                    dve.wait_ge(d_ready, i + 1)
                    dve.scalar_tensor_tensor(e[:], z_t[:], 1.0, d[:], ALU.add, ALU.mult).then_inc(e_ready, 1)
                    dve.wait_ge(e_ready, i + 1)
                    dve.scalar_tensor_tensor(yT[:], xT[b][:], 4.0, e[:], ALU.mult, ALU.subtract)\
                        .then_inc(y_ready, 1)
                if previous:
                    dve.wait_ge(gin_done, i)
                    dve.wait_ge(x1b_ready, i)
                    dve.tensor_tensor(y2[:], ps[:, DA, :].rearrange("c (t f) -> c t f", t=TILES), x1b[:], ALU.add)\
                        .then_inc(y2_ready, 1)
                    dve.wait_ge(y2_ready, i)
                    for t in range(TILES):
                        ins = dve.bn_stats(st2[:, t, :], y2[:, t, :])
                    ins.then_inc(ln2_stats, 1)
                    dve.wait_ge(ln2_stats, i)
                    join_halves(i, st2, mean2, half2, sq2, var2, LN_EPS, ln2_sums, ln2_terms, ln2_var)
                if following and not current:
                    for n in range(2, len(WAVES)):
                        split_wave(n)
                    dve.wait_ge(ident_ready, 1)
                    dve.wait_ge(pads_ready, 1)
                    for k in range(BP):
                        for q in range(2):
                            ins = dve.tensor_scalar(diag[:, k, q, q, :], ident[:], eps1[:, 0:1], None, ALU.mult)
                    ins.then_inc(eps_ready, 1)
                    dve.wait_ge(eps_ready, 1)
                if following:
                    dve.wait_ge(sum_conv_done, i + 2)
                    x_v = xT[1 - b][:].rearrange("c (b p m) -> c b p m", b=BP, p=2)
                    s_v = ps[:, CA, 0:BP * M].rearrange("c (b m) -> c b m", b=BP)
                    for p in range(2):
                        ins = dve.scalar_tensor_tensor(base[:, :, p, :], s_v, bn_shift[:, 1:2],
                                                       x_v[:, :, p, :], ALU.add, ALU.add)
                    ins.then_inc(base_ready, 1)

            def split_wave(n):
                bank, first, blocks = WAVES[n]
                dve.wait_ge(w_hi_ready, n + 1)
                dve.tensor_tensor(w_lo[:, first:first + blocks, :], ps[:, bank, 0:blocks * P],
                                  w_hi[:, first:first + blocks, :].bitcast(F32), ALU.subtract).then_inc(w_split, 1)

            iteration(-1, 1, False, False, True)
            iteration(0, 0, False, True, True)
            with dve.Fori(1, PAIRS - 2, 2) as t:
                iteration(t, 1, True, True, True)
                iteration(t + 1, 0, True, True, True)
            iteration(PAIRS - 1, 1, True, True, False)
            iteration(PAIRS, 0, True, False, False)

        @block.tensor
        def _(pe):
            def split_product(dst, block_, moving_hi, moving_lo, start, stop):
                pe.matmul(dst, w_hi[:, block_, :], moving_hi, start=start, stop=False)
                pe.matmul(dst, w_hi[:, block_, :], moving_lo, start=False, stop=False)
                return pe.matmul(dst, w_lo[:, block_, :], moving_hi, start=False, stop=stop)

            def parity_conv(dst, blocks, part, first, end):
                for a in range(first, end):
                    ins = split_product(dst, blocks[a], hs_hi[:, part, :, a:a + M], hs_lo[:, part, :, a:a + M],
                                        a == 0, a == len(blocks) - 1)
                return ins

            sum_taps = [SUM + a for a in range(ODD)] + [TAP + TAPS - 1]
            even_taps = [TAP + 2 * a for a in range(EVEN)]
            odd_taps = [TAP + 2 * a + 1 for a in range(ODD)]
            ca = ps[:, CA, 0:BP * M].rearrange("c (b m) -> c b m", b=BP)
            cb = ps[:, CB, :].rearrange("c (b p m) -> c b p m", b=BP, p=2)

            def turn_wave(n):
                bank, first, blocks = WAVES[n]
                for k in range(blocks):
                    block_ = first + k
                    if block_ < TAP:
                        natural = sums_nat[:, :, block_ - SUM]
                    elif block_ < GATE:
                        natural = conv2_nat[:, :, block_ - TAP]
                    else:
                        source, g = divmod(block_ - GATE, 3)
                        natural = hh_nat[:, g, :] if source == FROM_X else ih_nat[:, g, source * D:(source + 1) * D]
                    ins = pe.transpose(ps[:, bank, k * P:(k + 1) * P], natural, ident[:])
                ins.then_inc(w_turned, 1)

            def iteration(i, b, previous, current, following):
                if current:
                    if not previous:
                        pe.wait_ge(w_split, TAPS_SPLIT)
                    pe.wait_ge(u1_ready, i + 1)
                    parity_conv(ca, sum_taps, 0, 0, EVEN).then_inc(sum_conv_done, 1)
                    pe.wait_ge(diff_ready, i + 1)
                    pe.wait_ge(msg_added, i + 1)
                    parity_conv(cb[:, :, 0, :], even_taps, 1, 0, 4)
                    pe.wait_ge(lr_built, i + 1)
                    for t in range(TILES):
                        ins = pe.transpose(ps[:, DB, t * P:(t + 1) * P], lr[:, t, :].bitcast(F32), ident[:])
                    ins.then_inc(lr_turned, 1)
                if previous:
                    pe.wait_ge(y_ready, i)
                    for t in range(TILES):
                        ins = pe.transpose(ps[:, GR, t * P:(t + 1) * P], yT[:, t * P:(t + 1) * P], ident[:])
                    ins.then_inc(y_turned, 1)
                if current:
                    parity_conv(cb[:, :, 0, :], even_taps, 1, 4, EVEN)
                    pe.wait_ge(rows_ready, i + 1)
                    pe.wait_ge(base_ready, i + 1)
                    for k in range(BP):
                        for q in range(2):
                            m0 = (2 * k + q) * P
                            ins = pe.matmul(ps[:, DA + k, q * N:(q + 1) * N], left[:, m0:m0 + P],
                                            right[:, k * N:(k + 1) * N], start=True, stop=True)
                    ins.then_inc(dist_done, 1)
                    parity_conv(cb[:, :, 1, :], odd_taps, 2, 0, 4)
                    pe.wait_ge(adj_loaded, 16 * (i + 1))
                    pe.wait_ge(exp_ready, i + 1)
                    for k in range(BP):
                        for q in range(2):
                            for p in range(2):
                                c0 = (2 * q + p) * P
                                ins = pe.transpose(ps[:, DA + k, c0:c0 + P], adj_nat[:, k, p, q::2], ident[:])
                    ins.then_inc(adj_turned, 1)
                    parity_conv(cb[:, :, 1, :], odd_taps, 2, 4, ODD).then_inc(conv2_done, 1)
                    if not previous:
                        pe.wait_ge(w_split, GATES_SPLIT)
                    split_product(ps[:, GZ, :], GATE + 3 * FROM_X + GATE_Z, x_hi[:], x_lo[:], True, False)
                    split_product(ps[:, GNH, :], GATE + 3 * FROM_X + GATE_N, x_hi[:], x_lo[:], True, True)
                if previous:
                    pe.wait_ge(x1_ready, i)
                    for k in range(BP):
                        for q in range(2):
                            ins = pe.matmul(ps[:, CA, k * N:(k + 1) * N], x1[:, 2 * k + q, :],
                                            adjT[1 - b][:, k, q * N:(q + 1) * N], start=(q == 0), stop=(q == 1))
                    ins.then_inc(agg_done, 1)
                if current:
                    pe.wait_ge(msg_ready, i + 1)
                    pe.wait_ge(amask_ready, i + 1)
                    for k in range(BP):
                        for q in range(2):
                            ins = pe.matmul(ps[:, GNI, k * N:(k + 1) * N], msg[:, 2 * k + q, :],
                                            amask[:, k, q * N:(q + 1) * N], start=(q == 0), stop=(q == 1))
                    ins.then_inc(xn_done, 1)
                    split_product(ps[:, GR, :], GATE + 3 * FROM_X + GATE_R, x_hi[:], x_lo[:], True, False)
                    pe.wait_ge(adjT_ready, i + 1)
                if previous:
                    pe.wait_ge(gin_split, 1)
                    pe.wait_ge(h_ready, i)
                    for h, done in ((0, hidden0_done), (1, hidden1_done)):
                        cols = slice(h * P, (h + 1) * P)
                        pe.matmul(ps[:, DA + h, :], gin1_hi[:, cols], h_hi[:], start=True, stop=False)
                        pe.matmul(ps[:, DA + h, :], gin1_hi[:, cols], h_lo[:], start=False, stop=False)
                        pe.matmul(ps[:, DA + h, :], gin1_lo[:, cols], h_hi[:], start=False, stop=True)\
                            .then_inc(done, 1)
                if following:
                    pe.wait_ge(x_loaded, 16 * (i + 2))
                    for t in range(TILES):
                        ins = pe.transpose(ps[:, CA, t * P:(t + 1) * P], x_nat[:, t // 2, t % 2, :], ident[:])
                    ins.then_inc(x_turned, 1)
                if current:
                    pe.wait_ge(xn_ready, i + 1)
                    split_product(ps[:, GR, :], GATE + 3 * FROM_NMP + GATE_R, xn_hi[:], xn_lo[:], False, False)
                    split_product(ps[:, GZ, :], GATE + 3 * FROM_NMP + GATE_Z, xn_hi[:], xn_lo[:], False, False)
                    split_product(ps[:, GNI, :], GATE + 3 * FROM_NMP + GATE_N, xn_hi[:], xn_lo[:], True, False)
                    pe.wait_ge(xc_ready, i + 1)
                    for g, bank, done in ((GATE_R, GR, r_done), (GATE_N, GNI, n_done), (GATE_Z, GZ, z_done)):
                        split_product(ps[:, bank, :], GATE + 3 * FROM_CONV + g, xc_hi[:], xc_lo[:], False, True)\
                            .then_inc(done, 1)
                if following:
                    if not current:
                        pe.wait_ge(conv1_split, 1)
                    pe.wait_ge(x_ready, i + 2)
                    pe.matmul(ps[:, CA, :], conv1_hi[:], x_hi[:], start=True, stop=False)
                    pe.matmul(ps[:, CA, :], conv1_hi[:], x_lo[:], start=False, stop=False)
                    pe.matmul(ps[:, CA, :], conv1_lo[:], x_hi[:], start=False, stop=True).then_inc(conv1_done, 1)
                if previous:
                    pe.wait_ge(hidden_ready, i)
                    for t in range(TILES):
                        for h in range(2):
                            ins = pe.matmul(ps[:, DA, t * P:(t + 1) * P], hidden[:, h, t * P:(t + 1) * P],
                                            gin2[:, h, :], start=(h == 0), stop=(h == 1))
                    ins.then_inc(gin_done, 1)
                if following and not current:
                    pe.wait_ge(conv2_scaled, 1)
                    for n in range(2):
                        turn_wave(n)
                    pe.wait_ge(weights_loaded, 16 * N_BIG)
                    for n in range(2, 6):
                        turn_wave(n)
                    pe.wait_ge(w_split, 2)
                if following:
                    for t in range(TILES):
                        bank, c0 = (CB, DB)[t // 2], (t % 2) * SW
                        ins = pe.matmul(ps[:, bank, c0:c0 + SW], xT[1 - b][:, t * P:(t + 1) * P], msgse[:],
                                        start=True, stop=True)
                    ins.then_inc(msg_done, 1)

            pe.wait_ge(ident_ready, 1)
            pe.wait_ge(conv1_loaded, 16)
            pe.transpose(ps[:, CB, 0:P], conv1_nat[:], ident[:])
            pe.wait_ge(weights_loaded, 16 * N_BIG)
            pe.transpose(ps[:, CB, P:2 * P], msg_nat[:], ident[:])
            pe.transpose(ps[:, CB, 2 * P:2 * P + 3], se_nat[:], ident[0:3, 0:3]).then_inc(first_turned, 1)
            iteration(-1, 1, False, False, True)
            pe.wait_ge(w_split, 5)
            for n in range(6, len(WAVES)):
                turn_wave(n)
            iteration(0, 0, False, True, True)
            with pe.Fori(1, PAIRS - 2, 2) as t:
                iteration(t, 1, True, True, True)
                iteration(t + 1, 0, True, True, True)
            iteration(PAIRS - 1, 1, True, True, False)
            iteration(PAIRS, 0, True, False, False)


_INS = ['x', 'adj', 'L0_gnn_w_se', 'L0_gnn_b_se', 'L0_gnn_conv1_w', 'L0_gnn_bn1_g', 'L0_gnn_bn1_b', 'L0_gnn_bn1_m',
        'L0_gnn_bn1_v', 'L0_gnn_conv2_w', 'L0_gnn_bn2_g', 'L0_gnn_bn2_b', 'L0_gnn_bn2_m', 'L0_gnn_bn2_v',
        'L0_gnn_w_msg', 'L0_gnn_b_msg', 'L0_gnn_w_ih', 'L0_gnn_b_ih', 'L0_gnn_w_hh', 'L0_gnn_b_hh',
        'L1_gnn_eps', 'L1_gnn_W1', 'L1_gnn_b1', 'L1_gnn_W2', 'L1_gnn_b2']


def kernel(**inputs):
    import numpy as _np
    import concourse.bacc as _bacc
    from concourse import mybir as _mybir
    from concourse.bass_utils import run_bass_kernel_spmd as _run

    nc = _bacc.Bacc("TRN2", target_bir_lowering=False, num_devices=1)
    arrays, args = {}, []
    for name in _INS:
        a = _np.ascontiguousarray(inputs[name])
        arrays[f"in_{name}_dram"] = a
        args.append(nc.dram_tensor(f"in_{name}_dram", a.shape, _mybir.dt.from_np(a.dtype), kind="ExternalInput").ap())
    shape = tuple(inputs['x'].shape)
    args.append(nc.dram_tensor("out_0_dram", shape, _mybir.dt.float32, kind="ExternalOutput").ap())
    build_program(nc, *args)
    r = _run(nc, [arrays], core_ids=[0])
    return r.results[0]["out_0_dram"]
```

```python
import concourse.bass as bass
from concourse import mybir
from contextlib import ExitStack

F32 = mybir.dt.float32
F32R = mybir.dt.float32r
ALU = mybir.AluOpType
ACT = mybir.ActivationFunctionType

BN_EPS = 1e-5
LN_EPS = 1e-5


def build_program(nc, x, adj, w_se, b_se, conv1_w, bn1_g, bn1_b, bn1_m, bn1_v, conv2_w, bn2_g, bn2_b, bn2_m,
                  bn2_v, w_msg, b_msg, w_ih, b_ih, w_hh, b_hh, eps, W1, b1, W2, b2, out):
    B, N, D = x.shape
    HID = W1.shape[1]
    TAPS = conv2_w.shape[2]
    P = 128
    BP = 2
    PAIRS = B // BP
    M = N // 2
    T = BP * N
    TILES = T // P
    PAD = TAPS // 4
    MP = M + 2 * PAD
    EVEN, ODD = (TAPS + 1) // 2, TAPS // 2
    assert D == P and M == P and HID == 2 * P and TAPS == 17 and PAIRS % 2 == 0 and PAIRS >= 4

    SUM = 0
    EVEN_TAP = SUM + ODD
    ODD_TAP = EVEN_TAP + EVEN
    GATE = ODD_TAP + ODD
    BLOCKS = GATE + 9
    FROM_CONV, FROM_NMP, FROM_X = range(3)
    GATE_R, GATE_Z, GATE_N = range(3)
    S_ROWS = 24
    S_PAD = 32
    SW = P + 4

    x_pairs = x.rearrange("(i b) (m p) d -> i m b p d", b=BP, p=2)
    adj_pairs = adj.rearrange("(i b) (m p) c -> i m b p c", b=BP, p=2)
    out_pairs = out.rearrange("(i b) (m p) d -> i m b p d", b=BP, p=2)

    with ExitStack() as ctx:
        def sb(name, shape, dt=F32):
            return ctx.enter_context(nc.sbuf_tensor(name, shape, dt))

        def sem(name):
            return ctx.enter_context(nc.semaphore(name))

        ps = ctx.enter_context(nc.psum_tensor("ps", [P, 8, 512], F32))
        CA, CB, DA, DB, GR, GNH, GNI, GZ = range(8)

        ident = sb("ident", [P, P])
        conv1_nat = sb("conv1_nat", [P, D])
        conv2_nat = sb("conv2_nat", [P, D, TAPS])
        ih_nat = sb("ih_nat", [P, 3, 2 * D])
        hh_nat = sb("hh_nat", [P, 3, D])
        msg_nat = sb("msg_nat", [P, D])
        se_nat = sb("se_nat", [3, D])
        sums_nat = sb("sums_nat", [P, D, ODD])
        conv1_hi = sb("conv1_hi", [P, P], F32R)
        conv1_lo = sb("conv1_lo", [P, P], F32R)
        w_hi = sb("w_hi", [P, BLOCKS, P], F32R)
        w_lo = sb("w_lo", [P, BLOCKS, P], F32R)
        msgse = sb("msgse", [P, SW])
        gin1 = sb("gin1", [P, HID])
        gin1_hi = sb("gin1_hi", [P, HID], F32R)
        gin1_lo = sb("gin1_lo", [P, HID], F32R)
        gin2 = sb("gin2", [P, 2, D])
        bn = sb("bn", [P, 2, 4])
        bn_r = sb("bn_r", [P, 2])
        bn_scale = sb("bn_scale", [P, 2])
        bn_shift = sb("bn_shift", [P, 2])
        bn_t = sb("bn_t", [P, 2])
        bih = sb("bih", [P, 3])
        bhh = sb("bhh", [P, 3])
        b_rz = sb("b_rz", [P, 2])
        b_rs = sb("b_rs", [P, 1])
        b_zs = sb("b_zs", [P, 1])
        b1_col = sb("b1_col", [P, 2])
        eps_col = sb("eps_col", [P, 1])
        eps1 = sb("eps1", [P, 1])
        bmsg_row = sb("bmsg_row", [P, D])
        bse_row = sb("bse_row", [P, 3])
        b2_row = sb("b2_row", [P, D])
        diag = sb("diag", [P, BP, 2, 2, P])
        minus_half = sb("minus_half", [P, TILES])
        zeros = sb("zeros", [P, TILES, 6])

        x_nat = sb("x_nat", [P, BP, 2, D])
        adj_nat = sb("adj_nat", [P, BP, 2, N])
        xT = [sb(f"xT{k}", [P, T]) for k in range(2)]
        x_hi = sb("x_hi", [P, T], F32R)
        x_lo = sb("x_lo", [P, T], F32R)
        hs = sb("hs", [P, 4, BP, MP])
        hs_hi = sb("hs_hi", [P, 3, BP, MP], F32R)
        hs_lo = sb("hs_lo", [P, 3, BP, MP], F32R)
        msg_pre = sb("msg_pre", [P, TILES, D])
        msg_hi = sb("msg_hi", [P, TILES, D], F32R)
        msg_lo = sb("msg_lo", [P, TILES, D], F32R)
        s_nat = sb("s_nat", [P, TILES, 3])
        s_sq = sb("s_sq", [P, TILES, 3])
        lr = sb("lr", [P, TILES, P], F32R)
        left = sb("left", [S_ROWS, T], F32R)
        right = sb("right", [S_ROWS, T], F32R)
        expd = sb("expd", [P, BP, 512])
        amask = sb("amask", [P, BP, 512])
        amask_hi = sb("amask_hi", [P, BP, 512], F32R)
        amask_lo = sb("amask_lo", [P, BP, 512], F32R)
        adjT = sb("adjT", [P, BP, 512])
        adjT_hi = sb("adjT_hi", [P, BP, 512], F32R)
        adjT_lo = sb("adjT_lo", [P, BP, 512], F32R)
        x_shifted = sb("x_shifted", [P, T])
        base = sb("base", [P, BP, 2, M])
        conv_x = sb("conv_x", [P, T])
        xc_hi = sb("xc_hi", [P, T], F32R)
        xc_lo = sb("xc_lo", [P, T], F32R)
        xn_hi = sb("xn_hi", [P, T], F32R)
        xn_lo = sb("xn_lo", [P, T], F32R)
        r_t = sb("r_t", [P, T])
        z_t = sb("z_t", [P, T])
        r = sb("r", [P, T])
        u = sb("u", [P, T])
        w = sb("w", [P, T])
        n_t = sb("n_t", [P, T])
        d = sb("d", [P, T])
        e = sb("e", [P, T])
        yT = sb("yT", [P, T])
        st1 = sb("st1", [P, TILES, 6])
        mean1 = sb("mean1", [P, TILES])
        half1 = sb("half1", [P, TILES])
        sq1 = sb("sq1", [P, TILES])
        var1 = sb("var1", [P, TILES])
        rstd1 = sb("rstd1", [P, TILES])
        shift1 = sb("shift1", [P, TILES])
        neg_mean1 = sb("neg_mean1", [P, TILES])
        x1 = sb("x1", [P, TILES, D])
        x1_hi = sb("x1_hi", [P, TILES, D], F32R)
        x1_lo = sb("x1_lo", [P, TILES, D], F32R)
        x1b = sb("x1b", [P, TILES, D])
        h_hi = sb("h_hi", [P, T], F32R)
        h_lo = sb("h_lo", [P, T], F32R)
        hidden = sb("hidden", [P, 2, T])
        y2 = sb("y2", [P, TILES, D])
        st2 = sb("st2", [P, TILES, 6])
        mean2 = sb("mean2", [P, TILES])
        half2 = sb("half2", [P, TILES])
        sq2 = sb("sq2", [P, TILES])
        var2 = sb("var2", [P, TILES])
        rstd2 = sb("rstd2", [P, TILES])
        shift2 = sb("shift2", [P, TILES])
        neg_mean2 = sb("neg_mean2", [P, TILES])
        out_nat = sb("out_nat", [P, TILES, D])
        last_y2 = sb("last_y2", [P, TILES, D])
        last_out = sb("last_out", [P, TILES, D])

        ident_zero = sem("ident_zero")
        ident_ready = sem("ident_ready")
        msg_loaded = sem("msg_loaded")
        gates_loaded = sem("gates_loaded")
        gin_loaded = sem("gin_loaded")
        rows_loaded = sem("rows_loaded")
        columns_loaded = sem("columns_loaded")
        consts_ready = sem("consts_ready")
        pads_ready = sem("pads_ready")
        bn_loaded = sem("bn_loaded")
        conv1_loaded = sem("conv1_loaded")
        conv2_loaded = sem("conv2_loaded")
        bn_rsqrt = sem("bn_rsqrt")
        bn_scaled = sem("bn_scaled")
        bn_mean = sem("bn_mean")
        bn_var = sem("bn_var")
        eps_ready = sem("eps_ready")
        bias_summed = sem("bias_summed")
        taps_summed = sem("taps_summed")
        conv1_turned = sem("conv1_turned")
        msgse_turned = sem("msgse_turned")
        conv1_hi_ready = sem("conv1_hi_ready")
        conv1_split = sem("conv1_split")
        msgse_ready = sem("msgse_ready")
        w_turned = sem("w_turned")
        w_hi_ready = sem("w_hi_ready")
        w_split = sem("w_split")
        gin_hi_ready = sem("gin_hi_ready")
        gin_split = sem("gin_split")
        bn_ready = sem("bn_ready")
        setup_done = sem("setup_done")

        x_loaded = sem("x_loaded")
        adj_loaded = sem("adj_loaded")
        out_free = sem("out_free")
        x_turned = sem("x_turned")
        conv1_done = sem("conv1_done")
        msg_done = sem("msg_done")
        lr_turned = sem("lr_turned")
        sum_conv_done = sem("sum_conv_done")
        dist_done = sem("dist_done")
        adj_turned = sem("adj_turned")
        y_turned = sem("y_turned")
        conv2_done = sem("conv2_done")
        xn_done = sem("xn_done")
        agg_done = sem("agg_done")
        r_done = sem("r_done")
        z_done = sem("z_done")
        n_done = sem("n_done")
        hidden0_done = sem("hidden0_done")
        hidden1_done = sem("hidden1_done")
        gin_done = sem("gin_done")
        r_tanh = sem("r_tanh")
        z_tanh = sem("z_tanh")
        msg_hi_ready = sem("msg_hi_ready")
        amask_hi_ready = sem("amask_hi_ready")
        adjT_hi_ready = sem("adjT_hi_ready")
        x1_hi_ready = sem("x1_hi_ready")
        n_ready = sem("n_ready")
        rows_ready = sem("rows_ready")
        exp_ready = sem("exp_ready")
        x1_ready = sem("x1_ready")
        xc_hi_ready = sem("xc_hi_ready")
        xn_hi_ready = sem("xn_hi_ready")
        h_hi_ready = sem("h_hi_ready")
        hidden_ready = sem("hidden_ready")
        xT_ready = sem("xT_ready")
        x_shifted_ready = sem("x_shifted_ready")
        h1_ready = sem("h1_ready")
        out_ready = sem("out_ready")
        s_ready = sem("s_ready")
        msg_added = sem("msg_added")
        u_ready = sem("u_ready")
        w_ready = sem("w_ready")
        base_ready = sem("base_ready")
        last_d_ready = sem("last_d_ready")
        last_out_ready = sem("last_out_ready")
        e_ready = sem("e_ready")
        y_ready = sem("y_ready")
        ln1_stats = sem("ln1_stats")
        ln1_sums = sem("ln1_sums")
        ln1_terms = sem("ln1_terms")
        ln1_var = sem("ln1_var")
        msg_ready = sem("msg_ready")
        x1_lo_ready = sem("x1_lo_ready")
        masked = sem("masked")
        amask_ready = sem("amask_ready")
        adjT_ready = sem("adjT_ready")
        conv_added = sem("conv_added")
        xc_ready = sem("xc_ready")
        xn_ready = sem("xn_ready")
        h_ready = sem("h_ready")
        x_hi_ready = sem("x_hi_ready")
        x_ready = sem("x_ready")
        u1_hi_ready = sem("u1_hi_ready")
        u1_ready = sem("u1_ready")
        diffs_ready = sem("diffs_ready")
        diff_hi_ready = sem("diff_hi_ready")
        diff_ready = sem("diff_ready")
        y2_ready = sem("y2_ready")
        ln2_stats = sem("ln2_stats")
        ln2_sums = sem("ln2_sums")
        ln2_terms = sem("ln2_terms")
        ln2_var = sem("ln2_var")
        s_hi_ready = sem("s_hi_ready")
        s_lo_ready = sem("s_lo_ready")
        lr_built = sem("lr_built")
        r_ready = sem("r_ready")
        d_ready = sem("d_ready")
        ln1_rstd = sem("ln1_rstd")
        ln1_shift = sem("ln1_shift")
        adjT_lo_ready = sem("adjT_lo_ready")
        x1b_ready = sem("x1b_ready")
        ln2_rstd = sem("ln2_rstd")
        ln2_shift = sem("ln2_shift")

        WHOLE, HALVES = (0, BP), ((0, 1), (1, 1))

        def tiles_of(piece):
            return slice(2 * piece[0], 2 * (piece[0] + piece[1]))

        def tile_range(piece):
            return range(2 * piece[0], 2 * (piece[0] + piece[1]))

        def columns_of(piece):
            return slice(N * piece[0], N * (piece[0] + piece[1]))

        def bank_of(piece, whole, halves):
            return whole if piece == WHOLE else halves[piece[0]]

        def hidden_psum(piece, h):
            if piece == WHOLE:
                return ps[:, DA + h, :]
            return ps[:, DA + piece[0], h * N:(h + 1) * N]

        def y2_of(piece):
            return y2 if piece == WHOLE else last_y2

        N_ROWS, N_COLUMNS = 4, 3 + 3 + 2

        block = ctx.enter_context(nc.Block())

        @block.sync
        def _(sp):
            sp.dma_start(x_nat[:], x_pairs[0]).then_inc(x_loaded, 16)
            sp.dma_start(conv1_nat[:], conv1_w.rearrange("o i k -> o (i k)")).then_inc(conv1_loaded, 16)
            for k, vector in enumerate((bn1_v, bn1_g, bn1_b, bn1_m)):
                sp.dma_start(bn[:, 0, k:k + 1], vector.unsqueeze(1)).then_inc(bn_loaded, 16)
            sp.dma_start(msg_nat[:], w_msg).then_inc(msg_loaded, 16)
            sp.dma_start(se_nat[:], w_se).then_inc(msg_loaded, 16)
            sp.dma_start(ih_nat[:], w_ih.rearrange("(g o) i -> o g i", g=3)).then_inc(gates_loaded, 16)
            sp.dma_start(hh_nat[:], w_hh.rearrange("(g o) i -> o g i", g=3)).then_inc(gates_loaded, 16)
            sp.dma_start(adj_nat[:], adj_pairs[0]).then_inc(adj_loaded, 16)
            sp.dma_start(gin1[:], W1).then_inc(gin_loaded, 16)
            sp.dma_start(gin2[:], W2.rearrange("(h p) d -> p h d", h=2)).then_inc(gin_loaded, 16)
            for dst, vector in ((bih, b_ih), (bhh, b_hh), (b1_col, b1)):
                for k in range(vector.shape[0] // P):
                    sp.dma_start(dst[:, k:k + 1], vector[k * P:(k + 1) * P].unsqueeze(1))\
                        .then_inc(columns_loaded, 16)

            def load_x(i):
                sp.wait_ge(x_turned, i)
                sp.dma_start(x_nat[:], x_pairs[i]).then_inc(x_loaded, 16)

            def load_adj(i):
                sp.wait_ge(adj_turned, i)
                sp.dma_start(adj_nat[:], adj_pairs[i]).then_inc(adj_loaded, 16)

            def store(n):
                sp.wait_ge(out_ready, n)
                sp.dma_start(out_pairs[n - 1], out_nat[:].rearrange("p (b q) d -> p b q d", b=BP))\
                    .then_inc(out_free, 16)

            load_x(1)
            load_adj(1)
            load_x(2)
            with sp.Fori(1, PAIRS - 2) as t:
                load_adj(t + 1)
                load_x(t + 2)
                store(t)
            load_adj(PAIRS - 1)
            store(PAIRS - 2)
            store(PAIRS - 1)
            for k, ready in enumerate((out_ready, last_out_ready)):
                sp.wait_ge(ready, (PAIRS, 1)[k])
                sp.dma_start(out_pairs[PAIRS - 1][:, k], last_out[:, 2 * k:2 * k + 2, :]).then_inc(out_free, 16)
            sp.wait_ge(out_free, 16 * (PAIRS + 2))

        @block.gpsimd
        def _(pool):
            pool.memset(ident[:], 0.0).then_inc(ident_zero, 1)
            pool.memset(out_nat[:, 0, 0:1], 0.0).then_inc(out_free, 16)
            pool.wait_ge(ident_zero, 1)
            pool.affine_select(out=ident[:], in_=ident[:], compare_op=ALU.not_equal, fill=1.0, base=0,
                               pattern=[[-1, P]], channel_multiplier=1).then_inc(ident_ready, 1)
            pool.memset(msgse[:, P + 3:SW], 0.0)
            pool.memset(hs[:], 0.0).then_inc(pads_ready, 1)
            pool.memset(zeros[:], 0.0)
            pool.memset(minus_half[:], -0.5).then_inc(consts_ready, 1)
            for dst, vector in ((bse_row, b_se), (bmsg_row, b_msg), (b2_row, b2), (eps_col, eps)):
                pool.dma_start(dst[:], vector.partition_broadcast(P)).then_inc(rows_loaded, 16)
            pool.memset(lr[:].bitcast(F32), 0.0).then_inc(consts_ready, 1)
            pool.wait_ge(consts_ready, 2)
            pool.memset(lr[:, :, 18:24].bitcast(F32), 1.0).then_inc(consts_ready, 1)
            pool.memset(lr[:, :, S_PAD + 12:S_PAD + 18].bitcast(F32), 1.0).then_inc(consts_ready, 1)
            pool.wait_ge(consts_ready, 4)
            pool.wait_ge(bn_var, 1)
            pool.tensor_tensor(bn_r[:], bn_t[:], minus_half[:, 0:2], ALU.pow).then_inc(bn_rsqrt, 1)
            pool.memset(diag[:], 0.0).then_inc(pads_ready, 1)

            def build_lr(n):
                hi, lo = lr[:, :, 0:3], lr[:, :, 6:9]
                pool.wait_ge(s_ready, n)
                pool.tensor_tensor(s_sq[:], s_nat[:], s_nat[:], ALU.mult)
                pool.tensor_tensor(lr[:, :, 12:15], s_nat[:], s_nat[:], ALU.mult)
                pool.tensor_copy(hi, s_nat[:]).then_inc(s_hi_ready, 1)
                pool.wait_ge(s_hi_ready, n)
                pool.tensor_tensor(lo, s_nat[:], hi.bitcast(F32), ALU.subtract)
                pool.tensor_tensor(lr[:, :, 15:18], s_sq[:], lr[:, :, 12:15].bitcast(F32),
                                   ALU.subtract).then_inc(s_lo_ready, 1)
                pool.tensor_copy(lr[:, :, 3:6], hi.bitcast(F32))
                for at in (0, 6):
                    pool.tensor_scalar(lr[:, :, S_PAD + at:S_PAD + at + 3], hi.bitcast(F32), -2.0, 0.0,
                                       ALU.mult, ALU.add)
                pool.wait_ge(s_lo_ready, n)
                pool.tensor_tensor(lr[:, :, S_PAD + 18:S_PAD + 24], lr[:, :, 12:18].bitcast(F32),
                                   zeros[:], ALU.add)
                pool.tensor_copy(lr[:, :, 9:12], lo.bitcast(F32))
                for at in (3, 9):
                    ins = pool.tensor_scalar(lr[:, :, S_PAD + at:S_PAD + at + 3], lo.bitcast(F32), -2.0, 0.0,
                                             ALU.mult, ALU.add)
                ins.then_inc(lr_built, 1)

            def ln1_scale_shift(n, piece=WHOLE):
                ts = tiles_of(piece)
                pool.wait_ge(ln1_var, n)
                pool.tensor_tensor(neg_mean1[:, ts], mean1[:, ts], minus_half[:, ts], ALU.mult)
                pool.tensor_tensor(rstd1[:, ts], var1[:, ts], minus_half[:, ts], ALU.pow).then_inc(ln1_rstd, 1)
                pool.wait_ge(ln1_rstd, n)
                pool.tensor_tensor(shift1[:, ts], neg_mean1[:, ts], rstd1[:, ts], ALU.mult).then_inc(ln1_shift, 1)

            def add_b2(n, piece=WHOLE):
                ts = tiles_of(piece)
                pool.wait_ge(x1_ready, n)
                pool.tensor_tensor(x1b[:, ts], x1[:, ts],
                                   b2_row[:].unsqueeze(1).to_broadcast([P, 2 * piece[1], D]), ALU.add)\
                    .then_inc(x1b_ready, 1)

            def adjT_second(n):
                pool.wait_ge(adjT_hi_ready, n)
                pool.tensor_tensor(adjT_lo[:], adjT[:], adjT_hi[:].bitcast(F32), ALU.subtract)\
                    .then_inc(adjT_lo_ready, 1)

            def ln2_scale_shift(n, piece=WHOLE):
                ts = tiles_of(piece)
                pool.wait_ge(ln2_var, n)
                pool.tensor_tensor(neg_mean2[:, ts], mean2[:, ts], minus_half[:, ts], ALU.mult)
                pool.tensor_tensor(rstd2[:, ts], var2[:, ts], minus_half[:, ts], ALU.pow).then_inc(ln2_rstd, 1)
                pool.wait_ge(ln2_rstd, n)
                pool.tensor_tensor(shift2[:, ts], neg_mean2[:, ts], rstd2[:, ts], ALU.mult).then_inc(ln2_shift, 1)

            def iteration(i, b, previous, current, following):
                if previous:
                    add_b2(i)
                if current and following:
                    adjT_second(i + 1)
                    pool.wait_ge(n_ready, i + 1)
                    pool.tensor_tensor(d[:], xT[b][:], n_t[:], ALU.subtract).then_inc(d_ready, 1)
                if following:
                    build_lr(i + 2)
                if current and following:
                    ln1_scale_shift(i + 1)
                if previous and following:
                    ln2_scale_shift(i)

            iteration(-1, 1, False, False, True)
            pool.wait_ge(gin_loaded, 16 * 2)
            pool.tensor_copy(gin1_hi[:], gin1[:]).then_inc(gin_hi_ready, 1)
            pool.wait_ge(gin_hi_ready, 1)
            pool.tensor_tensor(gin1_lo[:], gin1[:], gin1_hi[:].bitcast(F32), ALU.subtract).then_inc(gin_split, 1)
            pool.wait_ge(rows_loaded, 16 * N_ROWS)
            iteration(0, 0, False, True, True)
            with pool.Fori(1, PAIRS - 2, 2) as t:
                iteration(t, 1, True, True, True)
                iteration(t + 1, 0, True, True, True)
            iteration(PAIRS - 1, 1, True, True, False)
            adjT_second(PAIRS)
            for k in range(BP):
                ln1_scale_shift(PAIRS + k, HALVES[k])
            pool.wait_ge(y2_ready, PAIRS - 1)
            for k in range(BP):
                add_b2(PAIRS + k, HALVES[k])
            ln2_scale_shift(PAIRS - 1)
            pool.wait_ge(out_ready, PAIRS - 1)
            for k in range(BP):
                ln2_scale_shift(PAIRS + k, HALVES[k])

        WAVES = [(2, 0, 4), (3, 4, 4), (4, 8, 4), (5, 12, 4), (6, 16, 4), (7, 20, 4),
                 (2, 24, 4), (4, 28, 4), (5, 32, 2)]
        assert sum(n for _, _, n in WAVES) == BLOCKS

        def waves_to(block_):
            return 1 + max(n for n, (_, first, _) in enumerate(WAVES) if first <= block_)

        @block.scalar
        def _(act):
            act.dma_start(conv2_nat[:], conv2_w).then_inc(conv2_loaded, 16)
            for k, vector in enumerate((bn2_v, bn2_g, bn2_b, bn2_m)):
                act.dma_start(bn[:, 1, k:k + 1], vector.unsqueeze(1)).then_inc(bn_loaded, 16)

            def ln1_apply(n, piece=WHOLE):
                bank, ts = bank_of(piece, GR, (GR, GNH)), tiles_of(piece)
                act.wait_ge(ln1_shift, n)
                for t in tile_range(piece):
                    ins = act.activation(x1[:, t, :], ps[:, bank, t * P:(t + 1) * P], ACT.Identity,
                                         bias=shift1[:, t:t + 1], scale=rstd1[:, t:t + 1])
                ins.then_inc(x1_ready, 1)
                act.wait_ge(x1_ready, n)
                act.activation(x1_hi[:, ts], x1[:, ts], ACT.Copy).then_inc(x1_hi_ready, 1)

            def adjT_first(n):
                act.wait_ge(adjT_ready, n)
                act.activation(adjT_hi[:], adjT[:], ACT.Copy).then_inc(adjT_hi_ready, 1)

            def agg_hi(n, piece=WHOLE):
                bank, cols = bank_of(piece, CA, (CA, CB)), columns_of(piece)
                act.wait_ge(agg_done, n)
                act.activation(h_hi[:, cols], ps[:, bank, cols], ACT.Copy).then_inc(h_hi_ready, 1)

            def gin_relu(n, piece=WHOLE):
                cols = columns_of(piece)
                act.wait_ge(hidden0_done if piece == WHOLE else hidden1_done, n)
                act.activation(hidden[:, 0, cols], hidden_psum(piece, 0), ACT.Relu, bias=b1_col[:, 0:1])
                act.wait_ge(hidden1_done, n)
                act.activation(hidden[:, 1, cols], hidden_psum(piece, 1), ACT.Relu, bias=b1_col[:, 1:2])\
                    .then_inc(hidden_ready, 1)

            def ln2_apply(n):
                act.wait_ge(ln2_shift, n)
                act.wait_ge(out_free, 16 * n)
                for t in range(TILES):
                    ins = act.activation(out_nat[:, t, :], y2[:, t, :], ACT.Identity,
                                         bias=shift2[:, t:t + 1], scale=rstd2[:, t:t + 1])
                ins.then_inc(out_ready, 1)

            def copy_x(i, b):
                act.wait_ge(x_turned, i + 2)
                act.activation(xT[1 - b][:], ps[:, CA, :], ACT.Copy).then_inc(xT_ready, 1)

            def first_conv_out(i, current):
                if not current:
                    for n in range(3):
                        copy_wave(n)
                    act.wait_ge(bn_ready, 1)
                    act.wait_ge(pads_ready, 1)
                act.wait_ge(conv1_done, i + 2)
                for p in range(2):
                    ins = act.activation(hs[:, p, :, PAD:PAD + M],
                                         ps[:, CA, :].rearrange("c (b p m) -> c b p m", b=BP, p=2)[:, :, p, :],
                                         ACT.Relu, bias=bn_shift[:, 0:1], scale=bn_scale[:, 0:1])
                ins.then_inc(h1_ready, 1)

            def iteration(i, b, previous, current, following):
                early = current and not previous
                if previous and following:
                    agg_hi(i)
                if early:
                    copy_x(i, b)
                if current:
                    act.wait_ge(xn_done, i + 1)
                    act.activation(xn_hi[:], ps[:, GNI, :], ACT.Copy).then_inc(xn_hi_ready, 1)
                    act.wait_ge(conv_added, i + 1)
                    act.activation(xc_hi[:], conv_x[:], ACT.Relu).then_inc(xc_hi_ready, 1)
                if current and not following:
                    agg_hi(i)
                    adjT_first(i + 1)
                if previous and following:
                    gin_relu(i)
                if following and not early:
                    copy_x(i, b)
                if current and following:
                    adjT_first(i + 1)
                if early:
                    first_conv_out(i, current)
                if current:
                    if not previous:
                        act.wait_ge(setup_done, 1)
                    act.wait_ge(r_done, i + 1)
                    act.activation(r_t[:], ps[:, GR, :], ACT.Tanh, bias=b_rs[:], scale=0.5).then_inc(r_tanh, 1)
                    act.wait_ge(z_done, i + 1)
                    act.activation(z_t[:], ps[:, GZ, :], ACT.Tanh, bias=b_zs[:], scale=-0.5)\
                        .then_inc(z_tanh, 1)
                if following and not early:
                    first_conv_out(i, current)
                if current:
                    act.wait_ge(w_ready, i + 1)
                    for piece in (WHOLE,) if following else HALVES:
                        cols = columns_of(piece)
                        act.activation(n_t[:, cols], w[:, cols], ACT.Tanh, bias=bih[:, GATE_N:GATE_N + 1])\
                            .then_inc(n_ready, 1)
                if following and not current:
                    act.wait_ge(msgse_turned, 1)
                    act.activation(msgse[:, 0:P + 3], ps[:, CB, 0:P + 3], ACT.Copy).then_inc(msgse_ready, 1)
                    for n in range(3, 6):
                        copy_wave(n)
                if following:
                    act.wait_ge(xT_ready, i + 2)
                    act.activation(x_shifted[:], xT[1 - b][:], ACT.Identity, bias=bn_shift[:, 1:2])\
                        .then_inc(x_shifted_ready, 1)
                    act.wait_ge(msg_added, i + 2)
                    act.activation(msg_hi[:], msg_pre[:], ACT.Relu).then_inc(msg_hi_ready, 1)
                    if not current:
                        for n in range(6, len(WAVES)):
                            copy_wave(n)
                    act.wait_ge(lr_turned, i + 2)
                    act.activation(left[:], ps[0:S_ROWS, DB, :], ACT.Copy)
                    act.activation(right[:], ps[S_PAD:S_PAD + S_ROWS, DB, :], ACT.Copy).then_inc(rows_ready, 1)
                    act.wait_ge(dist_done, i + 2)
                    act.activation(expd[:], ps[:, DA:DB + 1, :], ACT.Exp, scale=-1.0).then_inc(exp_ready, 1)
                if current and following:
                    ln1_apply(i + 1)
                if following:
                    act.wait_ge(masked, i + 2)
                    act.activation(amask_hi[:], amask[:], ACT.Copy).then_inc(amask_hi_ready, 1)
                if previous and following:
                    ln2_apply(i)

            def copy_wave(n):
                bank, first, blocks = WAVES[n]
                act.wait_ge(w_turned, n + 1)
                act.activation(w_hi[:, first:first + blocks, :], ps[:, bank, 0:blocks * P], ACT.Copy)\
                    .then_inc(w_hi_ready, 1)

            act.wait_ge(conv1_turned, 1)
            act.activation(conv1_hi[:], ps[:, CB, 0:P], ACT.Copy).then_inc(conv1_hi_ready, 1)
            iteration(-1, 1, False, False, True)
            iteration(0, 0, False, True, True)
            with act.Fori(1, PAIRS - 2, 2) as t:
                iteration(t, 1, True, True, True)
                iteration(t + 1, 0, True, True, True)
            iteration(PAIRS - 1, 1, True, True, False)
            gin_relu(PAIRS - 1)
            for k in range(BP):
                ln1_apply(PAIRS + k, HALVES[k])
            for k in range(BP):
                agg_hi(PAIRS + k, HALVES[k])
            for k in range(BP):
                gin_relu(PAIRS + k, HALVES[k])
            ln2_apply(PAIRS - 1)
            act.wait_ge(ln2_shift, PAIRS)
            for t in tile_range(HALVES[0]):
                ins = act.activation(last_out[:, t, :], last_y2[:, t, :], ACT.Identity,
                                     bias=shift2[:, t:t + 1], scale=rstd2[:, t:t + 1])
            ins.then_inc(out_ready, 1)

        @block.vector
        def _(dve):
            dve.wait_ge(conv2_loaded, 16)
            dve.tensor_tensor(sums_nat[:], conv2_nat[:, :, 0:2 * ODD:2], conv2_nat[:, :, 1:2 * ODD:2], ALU.add)\
                .then_inc(taps_summed, 1)
            dve.wait_ge(bn_loaded, 16 * 8)
            dve.tensor_scalar(bn_t[:], bn[:, :, 0], BN_EPS, None, ALU.add).then_inc(bn_var, 1)
            dve.wait_ge(conv1_hi_ready, 1)
            dve.tensor_tensor(conv1_lo[:], ps[:, CB, 0:P], conv1_hi[:].bitcast(F32), ALU.subtract)\
                .then_inc(conv1_split, 1)

            def join_halves(n, ts, st, mean, half, sq, var, eps_, sums, terms, done):
                dve.tensor_tensor(mean[:, ts], st[:, ts, 1], st[:, ts, 4], ALU.add)
                dve.tensor_tensor(half[:, ts], st[:, ts, 1], st[:, ts, 4], ALU.subtract)
                dve.tensor_tensor(var[:, ts], st[:, ts, 2], st[:, ts, 5], ALU.add).then_inc(sums, 1)
                dve.wait_ge(sums, n)
                dve.tensor_tensor(sq[:, ts], half[:, ts], half[:, ts], ALU.mult)
                dve.tensor_scalar(var[:, ts], var[:, ts], 1.0 / D, eps_, ALU.mult, ALU.add).then_inc(terms, 1)
                dve.wait_ge(terms, n)
                dve.scalar_tensor_tensor(var[:, ts], sq[:, ts], 0.25, var[:, ts], ALU.mult, ALU.add)\
                    .then_inc(done, 1)

            def ln1_statistics(n, piece=WHOLE):
                bank = bank_of(piece, GR, (GR, GNH))
                dve.wait_ge(y_turned, n)
                for t in tile_range(piece):
                    ins = dve.bn_stats(st1[:, t, :], ps[:, bank, t * P:(t + 1) * P])
                ins.then_inc(ln1_stats, 1)
                dve.wait_ge(ln1_stats, n)
                join_halves(n, tiles_of(piece), st1, mean1, half1, sq1, var1, 4 * LN_EPS,
                            ln1_sums, ln1_terms, ln1_var)

            def x1_second(n, piece=WHOLE):
                ts = tiles_of(piece)
                dve.wait_ge(x1_hi_ready, n)
                dve.tensor_tensor(x1_lo[:, ts], x1[:, ts], x1_hi[:, ts].bitcast(F32), ALU.subtract)\
                    .then_inc(x1_lo_ready, 1)

            def agg_lo(n, piece=WHOLE):
                bank, cols = bank_of(piece, CA, (CA, CB)), columns_of(piece)
                dve.wait_ge(h_hi_ready, n)
                dve.tensor_tensor(h_lo[:, cols], ps[:, bank, cols], h_hi[:, cols].bitcast(F32), ALU.subtract)\
                    .then_inc(h_ready, 1)

            def ln2_residual(n, piece=WHOLE):
                bank, ts = bank_of(piece, DA, (GNI, GZ)), tiles_of(piece)
                dve.wait_ge(gin_done, n)
                dve.wait_ge(x1b_ready, n)
                dve.tensor_tensor(y2_of(piece)[:, ts], ps[:, bank, :].rearrange("c (t f) -> c t f", t=TILES)[:, ts],
                                  x1b[:, ts], ALU.add).then_inc(y2_ready, 1)

            def ln2_statistics(n, piece=WHOLE):
                dve.wait_ge(y2_ready, n)
                for t in tile_range(piece):
                    ins = dve.bn_stats(st2[:, t, :], y2_of(piece)[:, t, :])
                ins.then_inc(ln2_stats, 1)
                dve.wait_ge(ln2_stats, n)
                join_halves(n, tiles_of(piece), st2, mean2, half2, sq2, var2, LN_EPS, ln2_sums, ln2_terms, ln2_var)

            def split_x(i, b):
                dve.wait_ge(xT_ready, i + 2)
                dve.tensor_copy(x_hi[:], xT[1 - b][:]).then_inc(x_hi_ready, 1)
                dve.wait_ge(x_hi_ready, i + 2)
                dve.tensor_tensor(x_lo[:], xT[1 - b][:], x_hi[:].bitcast(F32), ALU.subtract)\
                    .then_inc(x_ready, 1)

            def split_u1(i):
                dve.wait_ge(h1_ready, i + 2)
                dve.tensor_copy(hs_hi[:, 0], hs[:, 1]).then_inc(u1_hi_ready, 1)
                dve.wait_ge(u1_hi_ready, i + 2)
                dve.tensor_tensor(hs_lo[:, 0], hs[:, 1], hs_hi[:, 0].bitcast(F32), ALU.subtract)\
                    .then_inc(u1_ready, 1)

            def iteration(i, b, previous, current, following):
                early = current and not previous
                if current:
                    dve.wait_ge(msg_hi_ready, i + 1)
                    dve.scalar_tensor_tensor(msg_lo[:], msg_pre[:], 0.0, msg_hi[:].bitcast(F32), ALU.max,
                                             ALU.subtract).then_inc(msg_ready, 1)
                    dve.wait_ge(adj_turned, i + 1)
                    dve.tensor_tensor(amask[:], ps[:, DA:DB + 1, :], expd[:], ALU.mult).then_inc(masked, 1)
                if previous and following:
                    x1_second(i)
                if current:
                    if previous:
                        dve.wait_ge(adjT_lo_ready, i)
                    dve.tensor_tensor(adjT[:], ps[:, DA:DB + 1, :],
                                      diag[:].rearrange("c b q p m -> c b (q p m)"), ALU.add)\
                        .then_inc(adjT_ready, 1)
                    dve.wait_ge(amask_hi_ready, i + 1)
                    dve.tensor_tensor(amask_lo[:], amask[:], amask_hi[:].bitcast(F32), ALU.subtract)\
                        .then_inc(amask_ready, 1)
                if previous and following:
                    agg_lo(i)
                elif previous:
                    x1_second(i)
                if current:
                    dve.wait_ge(conv2_done, i + 1)
                    dve.scalar_tensor_tensor(conv_x[:], ps[:, CB, :], bn_scale[:, 1:2],
                                             base[:].rearrange("c b p m -> c (b p m)"), ALU.mult, ALU.add)\
                        .then_inc(conv_added, 1)
                if early:
                    split_x(i, b)
                if current:
                    dve.wait_ge(xn_hi_ready, i + 1)
                    dve.tensor_tensor(xn_lo[:], ps[:, GNI, :], xn_hi[:].bitcast(F32), ALU.subtract)\
                        .then_inc(xn_ready, 1)
                    dve.wait_ge(xc_hi_ready, i + 1)
                    dve.scalar_tensor_tensor(xc_lo[:], conv_x[:], 0.0, xc_hi[:].bitcast(F32), ALU.max,
                                             ALU.subtract).then_inc(xc_ready, 1)
                if current and not following:
                    agg_lo(i)
                if following and not early:
                    split_x(i, b)
                if following and not current:
                    dve.wait_ge(bn_rsqrt, 1)
                    dve.tensor_tensor(bn_scale[:], bn[:, :, 1], bn_r[:], ALU.mult).then_inc(bn_scaled, 1)
                    dve.wait_ge(bn_scaled, 1)
                    dve.tensor_tensor(bn_t[:], bn[:, :, 3], bn_scale[:], ALU.mult).then_inc(bn_mean, 1)
                    dve.wait_ge(bn_mean, 1)
                    dve.tensor_tensor(bn_shift[:], bn[:, :, 2], bn_t[:], ALU.subtract).then_inc(bn_ready, 1)
                    for n in range(3):
                        split_wave(n)
                if early:
                    split_u1(i)
                if current:
                    dve.wait_ge(r_tanh, i + 1)
                    dve.tensor_scalar(r[:], r_t[:], 0.5, 0.5, ALU.mult, ALU.add).then_inc(r_ready, 1)
                    dve.wait_ge(r_ready, i + 1)
                    dve.scalar_tensor_tensor(u[:], ps[:, GNH, :], bhh[:, GATE_N:GATE_N + 1], r[:], ALU.add,
                                             ALU.mult).then_inc(u_ready, 1)
                    dve.wait_ge(n_done, i + 1)
                    dve.wait_ge(u_ready, i + 1)
                    dve.tensor_tensor(w[:], ps[:, GNI, :], u[:], ALU.add).then_inc(w_ready, 1)
                if following:
                    if not early:
                        split_u1(i)
                    if not current:
                        dve.wait_ge(rows_loaded, 16 * N_ROWS)
                    dve.tensor_tensor(hs[:, 2], hs[:, 0], hs[:, 1], ALU.subtract)
                    dve.tensor_tensor(hs[:, 3, :, 0:MP - 1], hs[:, 0, :, 1:MP], hs[:, 1, :, 0:MP - 1],
                                      ALU.subtract).then_inc(diffs_ready, 1)
                    tiles = ps[:, CB:DB + 1:2, 0:2 * SW].rearrange("c k (t f) -> c k t f", t=2)
                    dve.wait_ge(msg_done, i + 2)
                    dve.tensor_tensor(s_nat[:].rearrange("c (k t) f -> c k t f", k=2), tiles[:, :, :, P:P + 3],
                                      bse_row[:].unsqueeze(1).unsqueeze(1).to_broadcast([P, 2, 2, 3]), ALU.add)\
                        .then_inc(s_ready, 1)
                    dve.wait_ge(diffs_ready, i + 2)
                    dve.tensor_copy(hs_hi[:, 1:3], hs[:, 2:4]).then_inc(diff_hi_ready, 1)
                    dve.wait_ge(diff_hi_ready, i + 2)
                    dve.tensor_tensor(hs_lo[:, 1:3], hs[:, 2:4], hs_hi[:, 1:3].bitcast(F32), ALU.subtract)\
                        .then_inc(diff_ready, 1)
                    dve.tensor_tensor(msg_pre[:].rearrange("c (k t) f -> c k t f", k=2), tiles[:, :, :, 0:P],
                                      bmsg_row[:].unsqueeze(1).unsqueeze(1).to_broadcast([P, 2, 2, D]), ALU.add)\
                        .then_inc(msg_added, 1)
                if current:
                    dve.wait_ge(z_tanh, i + 1)
                if current and following:
                    dve.wait_ge(d_ready, i + 1)
                    dve.scalar_tensor_tensor(e[:], z_t[:], 1.0, d[:], ALU.add, ALU.mult).then_inc(e_ready, 1)
                    dve.wait_ge(e_ready, i + 1)
                    dve.scalar_tensor_tensor(yT[:], xT[b][:], 4.0, e[:], ALU.mult, ALU.subtract)\
                        .then_inc(y_ready, 1)
                if previous and following:
                    ln2_residual(i)
                if following and not current:
                    for n in range(3, 6):
                        split_wave(n)
                if following:
                    dve.wait_ge(sum_conv_done, i + 2)
                    dve.wait_ge(x_shifted_ready, i + 2)
                    x_v = x_shifted[:].rearrange("c (b p m) -> c b p m", b=BP, p=2)
                    s_v = ps[:, CA, 0:BP * M].rearrange("c (b m) -> c b m", b=BP)
                    for p in range(2):
                        ins = dve.scalar_tensor_tensor(base[:, :, p, :], s_v, bn_scale[:, 1:2],
                                                       x_v[:, :, p, :], ALU.mult, ALU.add)
                    ins.then_inc(base_ready, 1)
                if current and following:
                    ln1_statistics(i + 1)
                if previous and following:
                    ln2_statistics(i)
                if following and not current:
                    for n in range(6, len(WAVES)):
                        split_wave(n)
                    dve.wait_ge(columns_loaded, 16 * N_COLUMNS)
                    dve.tensor_tensor(b_rz[:], bih[:, 0:2], bhh[:, 0:2], ALU.add)
                    dve.tensor_scalar(eps1[:], eps_col[:], 1.0, None, ALU.add).then_inc(bias_summed, 1)
                    dve.wait_ge(bias_summed, 1)
                    dve.tensor_scalar(b_rs[:], b_rz[:, 0:1], 0.5, None, ALU.mult)
                    dve.tensor_scalar(b_zs[:], b_rz[:, 1:2], -0.5, None, ALU.mult).then_inc(setup_done, 1)
                    dve.wait_ge(ident_ready, 1)
                    dve.wait_ge(pads_ready, 2)
                    for k in range(BP):
                        for q in range(2):
                            ins = dve.tensor_scalar(diag[:, k, q, q, :], ident[:], eps1[:, 0:1], None, ALU.mult)
                    ins.then_inc(eps_ready, 1)
                    dve.wait_ge(eps_ready, 1)

            def split_wave(n):
                bank, first, blocks = WAVES[n]
                dve.wait_ge(w_hi_ready, n + 1)
                dve.tensor_tensor(w_lo[:, first:first + blocks, :], ps[:, bank, 0:blocks * P],
                                  w_hi[:, first:first + blocks, :].bitcast(F32), ALU.subtract).then_inc(w_split, 1)

            iteration(-1, 1, False, False, True)
            iteration(0, 0, False, True, True)
            with dve.Fori(1, PAIRS - 2, 2) as t:
                iteration(t, 1, True, True, True)
                iteration(t + 1, 0, True, True, True)
            iteration(PAIRS - 1, 1, True, True, False)
            for k in range(BP):
                cols = columns_of(HALVES[k])
                dve.wait_ge(n_ready, PAIRS + k)
                dve.tensor_tensor(d[:, cols], xT[1][:, cols], n_t[:, cols], ALU.subtract).then_inc(last_d_ready, 1)
                dve.wait_ge(last_d_ready, 1 + k)
                dve.scalar_tensor_tensor(e[:, cols], z_t[:, cols], 1.0, d[:, cols], ALU.add, ALU.mult)\
                    .then_inc(e_ready, 1)
                dve.wait_ge(e_ready, PAIRS + k)
                dve.scalar_tensor_tensor(yT[:, cols], xT[1][:, cols], 4.0, e[:, cols], ALU.mult, ALU.subtract)\
                    .then_inc(y_ready, 1)
            for k in range(BP):
                ln1_statistics(PAIRS + k, HALVES[k])
            x1_second(PAIRS, HALVES[0])
            ln2_residual(PAIRS - 1)
            x1_second(PAIRS + 1, HALVES[1])
            for k in range(BP):
                agg_lo(PAIRS + k, HALVES[k])
            ln2_statistics(PAIRS - 1)
            for k in range(BP):
                ln2_residual(PAIRS + k, HALVES[k])
                dve.wait_ge(ln2_shift, PAIRS - 1)
                ln2_statistics(PAIRS + k, HALVES[k])
            dve.wait_ge(ln2_shift, PAIRS + 1)
            for t in tile_range(HALVES[1]):
                ins = dve.tensor_scalar(last_out[:, t, :], last_y2[:, t, :], rstd2[:, t:t + 1], shift2[:, t:t + 1],
                                        ALU.mult, ALU.add)
            ins.then_inc(last_out_ready, 1)

        @block.tensor
        def _(pe):
            def split_product(dst, block_, moving_hi, moving_lo, start, stop):
                pe.matmul(dst, w_hi[:, block_, :], moving_hi, start=start, stop=False)
                pe.matmul(dst, w_hi[:, block_, :], moving_lo, start=False, stop=False)
                return pe.matmul(dst, w_lo[:, block_, :], moving_hi, start=False, stop=stop)

            def parity_conv(dst, blocks, part, first, end):
                for a in range(first, end):
                    ins = split_product(dst, blocks[a], hs_hi[:, part, :, a:a + M], hs_lo[:, part, :, a:a + M],
                                        a == 0, a == len(blocks) - 1)
                return ins

            sum_taps = [SUM + a for a in range(ODD)] + [EVEN_TAP]
            even_taps = [EVEN_TAP + 1 + a for a in range(EVEN - 1)] + [EVEN_TAP]
            odd_taps = [ODD_TAP + a for a in range(ODD)]
            ca = ps[:, CA, 0:BP * M].rearrange("c (b m) -> c b m", b=BP)
            cb = ps[:, CB, :].rearrange("c (b p m) -> c b p m", b=BP, p=2)

            def x_gates():
                split_product(ps[:, GZ, :], GATE + 3 * FROM_X + GATE_Z, x_hi[:], x_lo[:], True, False)
                split_product(ps[:, GNH, :], GATE + 3 * FROM_X + GATE_N, x_hi[:], x_lo[:], True, True)

            def x_reset_gate(i, previous):
                if previous:
                    pe.wait_ge(x1_ready, i)
                split_product(ps[:, GR, :], GATE + 3 * FROM_X + GATE_R, x_hi[:], x_lo[:], True, False)

            def turn_wave(n):
                bank, first, blocks = WAVES[n]
                for k in range(blocks):
                    block_ = first + k
                    if block_ < EVEN_TAP:
                        natural = sums_nat[:, :, block_ - SUM]
                    elif block_ == EVEN_TAP:
                        natural = conv2_nat[:, :, TAPS - 1]
                    elif block_ < ODD_TAP:
                        natural = conv2_nat[:, :, 2 * (block_ - EVEN_TAP - 1)]
                    elif block_ < GATE:
                        natural = conv2_nat[:, :, 2 * (block_ - ODD_TAP) + 1]
                    else:
                        source, g = divmod(block_ - GATE, 3)
                        natural = hh_nat[:, g, :] if source == FROM_X else ih_nat[:, g, source * D:(source + 1) * D]
                    ins = pe.transpose(ps[:, bank, k * P:(k + 1) * P], natural, ident[:])
                ins.then_inc(w_turned, 1)

            def turn_y(n, piece=WHOLE):
                bank = bank_of(piece, GR, (GR, GNH))
                pe.wait_ge(y_ready, n)
                for t in tile_range(piece):
                    ins = pe.transpose(ps[:, bank, t * P:(t + 1) * P], yT[:, t * P:(t + 1) * P], ident[:])
                ins.then_inc(y_turned, 1)

            def batch_products(piece, bank, stationary_hi, stationary_lo, moving_hi, moving_lo):
                for k in range(piece[0], piece[0] + piece[1]):
                    for q in range(2):
                        dst, cols = ps[:, bank, k * N:(k + 1) * N], slice(q * N, (q + 1) * N)
                        hi, lo = stationary_hi[:, 2 * k + q, :], stationary_lo[:, 2 * k + q, :]
                        pe.matmul(dst, hi, moving_hi[:, k, cols], start=(q == 0), stop=False)
                        pe.matmul(dst, hi, moving_lo[:, k, cols], start=False, stop=False)
                        ins = pe.matmul(dst, lo, moving_hi[:, k, cols], start=False, stop=(q == 1))
                return ins

            def aggregate(n, piece=WHOLE):
                pe.wait_ge(x1_lo_ready, n)
                pe.wait_ge(adjT_lo_ready, n if piece == WHOLE else PAIRS)
                batch_products(piece, bank_of(piece, CA, (CA, CB)), x1_hi, x1_lo, adjT_hi, adjT_lo)\
                    .then_inc(agg_done, 1)

            def gin_hidden(n, piece=WHOLE):
                cols = columns_of(piece)
                pe.wait_ge(gin_split, 1)
                pe.wait_ge(h_ready, n)
                for h, done in ((0, hidden0_done), (1, hidden1_done)):
                    dst, out_cols = hidden_psum(piece, h), slice(h * P, (h + 1) * P)
                    pe.matmul(dst, gin1_hi[:, out_cols], h_hi[:, cols], start=True, stop=False)
                    pe.matmul(dst, gin1_hi[:, out_cols], h_lo[:, cols], start=False, stop=False)
                    pe.matmul(dst, gin1_lo[:, out_cols], h_hi[:, cols], start=False, stop=True).then_inc(done, 1)

            def gin_out(n, piece=WHOLE):
                bank = bank_of(piece, DA, (GNI, GZ))
                pe.wait_ge(hidden_ready, n)
                for t in tile_range(piece):
                    for h in range(2):
                        ins = pe.matmul(ps[:, bank, t * P:(t + 1) * P], hidden[:, h, t * P:(t + 1) * P],
                                        gin2[:, h, :], start=(h == 0), stop=(h == 1))
                ins.then_inc(gin_done, 1)

            def turn_x(i):
                pe.wait_ge(x_loaded, 16 * (i + 2))
                for t in range(TILES):
                    ins = pe.transpose(ps[:, CA, t * P:(t + 1) * P], x_nat[:, t // 2, t % 2, :], ident[:])
                ins.then_inc(x_turned, 1)

            def first_conv(i):
                pe.wait_ge(x_ready, i + 2)
                pe.matmul(ps[:, CA, :], conv1_hi[:], x_hi[:], start=True, stop=False)
                pe.matmul(ps[:, CA, :], conv1_hi[:], x_lo[:], start=False, stop=False)
                pe.matmul(ps[:, CA, :], conv1_lo[:], x_hi[:], start=False, stop=True).then_inc(conv1_done, 1)

            def iteration(i, b, previous, current, following):
                early = current and not previous
                if current:
                    if not previous:
                        pe.wait_ge(w_split, waves_to(EVEN_TAP))
                    pe.wait_ge(u1_ready, i + 1)
                    parity_conv(ca, sum_taps, 0, 0, EVEN).then_inc(sum_conv_done, 1)
                    if not previous:
                        pe.wait_ge(gates_loaded, 16 * 2)
                        pe.wait_ge(w_split, 4)
                        for n in range(6, len(WAVES)):
                            turn_wave(n)
                        pe.wait_ge(w_split, waves_to(EVEN_TAP + EVEN - 1))
                    pe.wait_ge(diff_ready, i + 1)
                    pe.wait_ge(msg_added, i + 1)
                    parity_conv(cb[:, :, 0, :], even_taps, 1, 0, 4)
                    pe.wait_ge(lr_built, i + 1)
                    for t in range(TILES):
                        ins = pe.transpose(ps[:, DB, t * P:(t + 1) * P], lr[:, t, :].bitcast(F32), ident[:])
                    ins.then_inc(lr_turned, 1)
                if previous:
                    turn_y(i)
                if current:
                    parity_conv(cb[:, :, 0, :], even_taps, 1, 4, EVEN)
                    if not previous:
                        pe.wait_ge(w_split, waves_to(ODD_TAP + ODD - 1))
                    pe.wait_ge(rows_ready, i + 1)
                    pe.wait_ge(base_ready, i + 1)
                    for k in range(BP):
                        for q in range(2):
                            m0 = (2 * k + q) * P
                            ins = pe.matmul(ps[:, DA + k, q * N:(q + 1) * N], left[:, m0:m0 + P],
                                            right[:, k * N:(k + 1) * N], start=True, stop=True)
                    ins.then_inc(dist_done, 1)
                    parity_conv(cb[:, :, 1, :], odd_taps, 2, 0, 4)
                    pe.wait_ge(adj_loaded, 16 * (i + 1))
                    pe.wait_ge(exp_ready, i + 1)
                    for k in range(BP):
                        for q in range(2):
                            for p in range(2):
                                c0 = (2 * q + p) * P
                                ins = pe.transpose(ps[:, DA + k, c0:c0 + P], adj_nat[:, k, p, q::2], ident[:])
                    ins.then_inc(adj_turned, 1)
                    parity_conv(cb[:, :, 1, :], odd_taps, 2, 4, ODD).then_inc(conv2_done, 1)
                    if not previous:
                        pe.wait_ge(w_split, waves_to(BLOCKS - 1))
                    x_gates()
                if previous and following:
                    aggregate(i)
                if current:
                    x_reset_gate(i, previous)
                if early:
                    turn_x(i)
                if current:
                    pe.wait_ge(msg_ready, i + 1)
                    pe.wait_ge(amask_ready, i + 1)
                    batch_products(WHOLE, GNI, msg_hi, msg_lo, amask_hi, amask_lo).then_inc(xn_done, 1)
                if current and not following:
                    aggregate(i)
                if current:
                    pe.wait_ge(adjT_ready, i + 1)
                if previous and following:
                    gin_hidden(i)
                if following and not early:
                    turn_x(i)
                elif early:
                    first_conv(i)
                if current:
                    pe.wait_ge(xn_ready, i + 1)
                    split_product(ps[:, GR, :], GATE + 3 * FROM_NMP + GATE_R, xn_hi[:], xn_lo[:], False, False)
                    split_product(ps[:, GZ, :], GATE + 3 * FROM_NMP + GATE_Z, xn_hi[:], xn_lo[:], False, False)
                    split_product(ps[:, GNI, :], GATE + 3 * FROM_NMP + GATE_N, xn_hi[:], xn_lo[:], True, False)
                    pe.wait_ge(xc_ready, i + 1)
                    for g, bank, done in ((GATE_R, GR, r_done), (GATE_N, GNI, n_done), (GATE_Z, GZ, z_done)):
                        split_product(ps[:, bank, :], GATE + 3 * FROM_CONV + g, xc_hi[:], xc_lo[:], False, True)\
                            .then_inc(done, 1)
                if following and not current:
                    pe.wait_ge(taps_summed, 1)
                    for n in range(2):
                        turn_wave(n)
                    pe.wait_ge(conv2_loaded, 16)
                    turn_wave(2)
                    pe.wait_ge(conv1_split, 1)
                if following and not early:
                    first_conv(i)
                if previous and following:
                    gin_out(i)
                if following and not current:
                    pe.wait_ge(msg_loaded, 16 * 2)
                    pe.transpose(ps[:, CB, 0:P], msg_nat[:], ident[:])
                    pe.transpose(ps[:, CB, P:P + 3], se_nat[:], ident[0:3, 0:3]).then_inc(msgse_turned, 1)
                    for n in range(3, 6):
                        turn_wave(n)
                    pe.wait_ge(msgse_ready, 1)
                    pe.wait_ge(w_split, 2)
                if following:
                    for t in range(TILES):
                        bank, c0 = (CB, DB)[t // 2], (t % 2) * SW
                        ins = pe.matmul(ps[:, bank, c0:c0 + SW], xT[1 - b][:, t * P:(t + 1) * P], msgse[:],
                                        start=True, stop=True)
                    ins.then_inc(msg_done, 1)

            pe.wait_ge(ident_ready, 1)
            pe.wait_ge(conv1_loaded, 16)
            pe.transpose(ps[:, CB, 0:P], conv1_nat[:], ident[:]).then_inc(conv1_turned, 1)
            iteration(-1, 1, False, False, True)
            iteration(0, 0, False, True, True)
            with pe.Fori(1, PAIRS - 2, 2) as t:
                iteration(t, 1, True, True, True)
                iteration(t + 1, 0, True, True, True)
            iteration(PAIRS - 1, 1, True, True, False)
            gin_hidden(PAIRS - 1)
            for k in range(BP):
                turn_y(PAIRS + k, HALVES[k])
            gin_out(PAIRS - 1)
            for k in range(BP):
                aggregate(PAIRS + k, HALVES[k])
            for k in range(BP):
                gin_hidden(PAIRS + k, HALVES[k])
            for k in range(BP):
                gin_out(PAIRS + k, HALVES[k])


_INS = ['x', 'adj', 'L0_gnn_w_se', 'L0_gnn_b_se', 'L0_gnn_conv1_w', 'L0_gnn_bn1_g', 'L0_gnn_bn1_b', 'L0_gnn_bn1_m',
        'L0_gnn_bn1_v', 'L0_gnn_conv2_w', 'L0_gnn_bn2_g', 'L0_gnn_bn2_b', 'L0_gnn_bn2_m', 'L0_gnn_bn2_v',
        'L0_gnn_w_msg', 'L0_gnn_b_msg', 'L0_gnn_w_ih', 'L0_gnn_b_ih', 'L0_gnn_w_hh', 'L0_gnn_b_hh',
        'L1_gnn_eps', 'L1_gnn_W1', 'L1_gnn_b1', 'L1_gnn_W2', 'L1_gnn_b2']


def kernel(**inputs):
    import numpy as _np
    import concourse.bacc as _bacc
    from concourse import mybir as _mybir
    from concourse.bass_utils import run_bass_kernel_spmd as _run

    nc = _bacc.Bacc("TRN2", target_bir_lowering=False, num_devices=1)
    arrays, args = {}, []
    for name in _INS:
        a = _np.ascontiguousarray(inputs[name])
        arrays[f"in_{name}_dram"] = a
        args.append(nc.dram_tensor(f"in_{name}_dram", a.shape, _mybir.dt.from_np(a.dtype), kind="ExternalInput").ap())
    shape = tuple(inputs['x'].shape)
    args.append(nc.dram_tensor("out_0_dram", shape, _mybir.dt.float32, kind="ExternalOutput").ap())
    build_program(nc, *args)
    r = _run(nc, [arrays], core_ids=[0])
    return r.results[0]["out_0_dram"]
```
